# Optimizing a Trainium2 kernel written in Bass

```python
import numpy as np
import jax
import jax.numpy as jnp

def _softmax(x, axis=-1):
    return jax.nn.softmax(x, axis=axis)

def _gelu(x):
    return jax.nn.gelu(x, approximate=True)

def _silu(x):
    return jax.nn.silu(x)

def _sigmoid(x):
    return jax.nn.sigmoid(x)

def _layernorm(x, axis=-1, eps=1e-05):
    m = jnp.mean(x, axis=axis, keepdims=True)
    v = jnp.var(x, axis=axis, keepdims=True)
    return (x - m) / jnp.sqrt(v + eps)

def _scatter_add(tgt, idx, src, axis=0):
    return tgt.at[idx].add(src)

def _segment_sum(src, seg, n):
    return jax.ops.segment_sum(src, seg, n)
kernel_name = 'mk_audio_tower_d1_tok_audfeat256_r4_0b7c6d'

def setup_inputs(seed: int=0):
    np.random.seed(seed)
    _w = jnp.asarray

    def _rec_inputs():
        import jax
        import jax.numpy as jnp
        _rk = jax.random.key(seed)
        x = jax.random.uniform(jax.random.fold_in(_rk, 1), (16, 4, 256), jnp.float32, 0.0, 0.999986)
        return x
    x = _rec_inputs()

    def _L0_tok_setup():
        import jax, jax.numpy as jnp
        import numpy as np
        T = 8
        key = jax.random.key(seed)
        ks = jax.random.split(key, 9)
        bs, dims, L, d = (16, 4, 512, 64)
        x = jax.random.uniform(ks[0], (bs, dims, L), dtype=jnp.float32)
        s_in = 1.0 / np.sqrt(dims)
        s_d = 1.0 / np.sqrt(d)
        W1 = jax.random.uniform(ks[1], (d, dims), minval=-s_in, maxval=s_in, dtype=jnp.float32)
        b1 = jax.random.uniform(ks[2], (d,), minval=-s_in, maxval=s_in, dtype=jnp.float32)
        W2 = jax.random.uniform(ks[3], (d, d), minval=-s_d, maxval=s_d, dtype=jnp.float32)
        b2 = jax.random.uniform(ks[4], (d,), minval=-s_d, maxval=s_d, dtype=jnp.float32)
        W3 = jax.random.uniform(ks[5], (d, dims), minval=-s_in, maxval=s_in, dtype=jnp.float32)
        b3 = jax.random.uniform(ks[6], (d,), minval=-s_in, maxval=s_in, dtype=jnp.float32)
        W4 = jax.random.uniform(ks[7], (d, d), minval=-s_d, maxval=s_d, dtype=jnp.float32)
        b4 = jax.random.uniform(ks[8], (d,), minval=-s_d, maxval=s_d, dtype=jnp.float32)
        return dict(x=x, W1=W1, b1=b1, W2=W2, b2=b2, W3=W3, b3=b3, W4=W4, b4=b4)
    _L0_tok_all = _L0_tok_setup()
    _L0_tok_in = {k: v for k, v in _L0_tok_all.items() if k in ('W1', 'b1', 'W2', 'b2', 'W3', 'b3', 'W4', 'b4')}
    del _L0_tok_all

    def _L0_attn_setup():
        import jax, jax.numpy as jnp
        import numpy as np
        N_HEADS, EMB, KQ = (8, 64, 64)
        BATCH, SEQ = (4, 512)
        key = jax.random.key(seed)
        ks = jax.random.split(key, 5)
        x = jax.random.normal(ks[0], (BATCH, SEQ, EMB), dtype=jnp.float32)
        key_matrices = 0.1 * jax.random.normal(ks[1], (N_HEADS, EMB, KQ), dtype=jnp.float32)
        query_matrices = 0.1 * jax.random.normal(ks[2], (N_HEADS, EMB, KQ), dtype=jnp.float32)
        value_in_matrices = 0.1 * jax.random.normal(ks[3], (N_HEADS, EMB, KQ), dtype=jnp.float32)
        value_out_matrices = 0.1 * jax.random.normal(ks[4], (N_HEADS, KQ, EMB), dtype=jnp.float32)
        return {'x': x, 'key_matrices': key_matrices, 'query_matrices': query_matrices, 'value_in_matrices': value_in_matrices, 'value_out_matrices': value_out_matrices}
    _L0_attn_all = _L0_attn_setup()
    _L0_attn_in = {k: v for k, v in _L0_attn_all.items() if k in ('key_matrices', 'query_matrices', 'value_in_matrices', 'value_out_matrices')}
    del _L0_attn_all

    def _L0_ffn_setup():
        import jax, jax.numpy as jnp
        import numpy as np
        NUM_EXPERTS = 8
        TOP_K = 2
        B, S, D = (8, 2048, 64)

        def _moe(tokens, router_w, w1, b1, w2, b2):
            N = tokens.shape[0]
            E = router_w.shape[0]
            logits = tokens.astype(jnp.float32) @ router_w.astype(jnp.float32).T
            probs = jax.nn.softmax(logits, axis=-1)
            rw, re = jax.lax.top_k(probs, TOP_K)
            if TOP_K > 1:
                rw = rw / jnp.maximum(rw.sum(-1, keepdims=True), 1e-12)
            rw = rw.astype(tokens.dtype)
            combine = jnp.zeros((N, E), tokens.dtype).at[jnp.arange(N)[:, None], re].set(rw)
            out = tokens
            for e in range(E):
                h = jax.nn.gelu(tokens @ w1[e] + b1[e], approximate=False)
                y = h @ w2[e] + b2[e]
                out = out + combine[:, e:e + 1] * y
            return out
        key = jax.random.key(seed)
        ks = jax.random.split(key, 4)
        scale = 1.0 / np.sqrt(D).astype(np.float32)
        return {'input_embeddings': jax.random.normal(ks[0], (B, S, D), jnp.float32), 'router_w': jax.random.normal(ks[1], (NUM_EXPERTS, D), jnp.float32) * scale, 'w1': jax.random.normal(ks[2], (NUM_EXPERTS, D, D), jnp.float32) * scale, 'b1': jnp.zeros((NUM_EXPERTS, D), jnp.float32), 'w2': jax.random.normal(ks[3], (NUM_EXPERTS, D, D), jnp.float32) * scale, 'b2': jnp.zeros((NUM_EXPERTS, D), jnp.float32)}
    _L0_ffn_all = _L0_ffn_setup()
    _L0_ffn_in = {k: v for k, v in _L0_ffn_all.items() if k in ('router_w', 'w1', 'b1', 'w2', 'b2')}
    del _L0_ffn_all
    return {'x': x, 'L0_tok_W1': _L0_tok_in['W1'], 'L0_tok_b1': _L0_tok_in['b1'], 'L0_tok_W2': _L0_tok_in['W2'], 'L0_tok_b2': _L0_tok_in['b2'], 'L0_tok_W3': _L0_tok_in['W3'], 'L0_tok_b3': _L0_tok_in['b3'], 'L0_tok_W4': _L0_tok_in['W4'], 'L0_tok_b4': _L0_tok_in['b4'], 'L0_attn_key_matrices': _L0_attn_in['key_matrices'], 'L0_attn_query_matrices': _L0_attn_in['query_matrices'], 'L0_attn_value_in_matrices': _L0_attn_in['value_in_matrices'], 'L0_attn_value_out_matrices': _L0_attn_in['value_out_matrices'], 'L0_ffn_router_w': _L0_ffn_in['router_w'], 'L0_ffn_w1': _L0_ffn_in['w1'], 'L0_ffn_b1': _L0_ffn_in['b1'], 'L0_ffn_w2': _L0_ffn_in['w2'], 'L0_ffn_b2': _L0_ffn_in['b2']}

def reference(x, L0_tok_W1, L0_tok_b1, L0_tok_W2, L0_tok_b2, L0_tok_W3, L0_tok_b3, L0_tok_W4, L0_tok_b4, L0_attn_key_matrices, L0_attn_query_matrices, L0_attn_value_in_matrices, L0_attn_value_out_matrices, L0_ffn_router_w, L0_ffn_w1, L0_ffn_b1, L0_ffn_w2, L0_ffn_b2):
    import jax
    import jax.numpy as jnp

    def _L0_tok_ref(x, W1, b1, W2, b2, W3, b3, W4, b4):
        import jax, jax.numpy as jnp
        import numpy as np
        T = 8
        a = jnp.einsum('bdl,od->blo', x, W1) + b1
        bs, L, d = a.shape
        zcol = jnp.zeros((bs, 1, d), a.dtype)
        shift_r = lambda v: jnp.concatenate([zcol, v[:, :-1]], axis=1)
        shift_l = lambda v: jnp.concatenate([v[:, 1:], zcol], axis=1)
        up = jnp.zeros_like(a)
        down = jnp.zeros_like(a)
        for _ in range(T):
            up = jax.nn.relu(a + shift_r(up) @ W2.T + b2)
            down = jax.nn.relu(a + shift_l(down) @ W2.T + b2)
        c = jnp.einsum('bdl,od->blo', x, W3) + b3
        miu = jax.nn.relu(c + (shift_r(up) @ W4.T + b4) + (shift_l(down) @ W4.T + b4))
        return miu

    def _L0_attn_ref(x, key_matrices, query_matrices, value_in_matrices, value_out_matrices):
        import jax, jax.numpy as jnp
        import numpy as np
        N_HEADS, EMB, KQ = (8, 64, 64)
        BATCH, SEQ = (4, 512)
        seq_len = x.shape[1]
        queries = jnp.einsum('ned,bse->nbsd', query_matrices, x)
        keys = jnp.einsum('ned,bse->nbsd', key_matrices, x)
        kq = jnp.einsum('nbjd,nbkd->nbjk', keys, queries)
        mask = jnp.triu(jnp.ones((seq_len, seq_len), dtype=bool), k=1)
        kq = jnp.where(mask, -jnp.inf, kq)
        attention_pattern = jax.nn.softmax(kq, axis=3)
        v = jnp.einsum('bjp,npd->nbjd', x, value_in_matrices)
        ctx = jnp.einsum('nbsj,nbjd->nbsd', attention_pattern, v)
        return jnp.einsum('nbsd,nde->bse', ctx, value_out_matrices)

    def _L0_ffn_ref(input_embeddings, router_w, w1, b1, w2, b2):
        import jax, jax.numpy as jnp
        import numpy as np
        NUM_EXPERTS = 8
        TOP_K = 2
        B, S, D = (8, 2048, 64)

        def _moe(tokens, router_w, w1, b1, w2, b2):
            N = tokens.shape[0]
            E = router_w.shape[0]
            logits = tokens.astype(jnp.float32) @ router_w.astype(jnp.float32).T
            probs = jax.nn.softmax(logits, axis=-1)
            rw, re = jax.lax.top_k(probs, TOP_K)
            if TOP_K > 1:
                rw = rw / jnp.maximum(rw.sum(-1, keepdims=True), 1e-12)
            rw = rw.astype(tokens.dtype)
            combine = jnp.zeros((N, E), tokens.dtype).at[jnp.arange(N)[:, None], re].set(rw)
            out = tokens
            for e in range(E):
                h = jax.nn.gelu(tokens @ w1[e] + b1[e], approximate=False)
                y = h @ w2[e] + b2[e]
                out = out + combine[:, e:e + 1] * y
            return out
        b, s, d = input_embeddings.shape
        tokens = input_embeddings.reshape(b * s, d)
        return _moe(tokens, router_w, w1, b1, w2, b2).reshape(b, s, d)
    h = _L0_tok_ref(x, L0_tok_W1, L0_tok_b1, L0_tok_W2, L0_tok_b2, L0_tok_W3, L0_tok_b3, L0_tok_W4, L0_tok_b4)
    h = h + _L0_attn_ref(_layernorm(h, axis=-1), L0_attn_key_matrices, L0_attn_query_matrices, L0_attn_value_in_matrices, L0_attn_value_out_matrices)
    h = h + _L0_ffn_ref(_layernorm(h, axis=-1), L0_ffn_router_w, L0_ffn_w1, L0_ffn_b1, L0_ffn_w2, L0_ffn_b2)
    return h

_drawn_inputs = setup_inputs


def setup_inputs(seed=0):
    import zlib

    import numpy as np

    out = dict(_drawn_inputs(seed))
    spreads = {'L0_ffn_b1': (0.0, 0.467), 'L0_ffn_b2': (0.0, 0.344)}
    factors = {}
    for name, (base, spread) in spreads.items():
        noise = np.random.default_rng([zlib.crc32(name.encode()), seed]).standard_normal(out[name].shape)
        drawn = base * np.exp(spread * noise) if base else spread * noise
        out[name] = jnp.asarray(drawn.astype(out[name].dtype))
    for name, factor in factors.items():
        out[name] = (out[name] * factor).astype(out[name].dtype)
    return out
```

```python
import numpy as np
from contextlib import ExitStack

import concourse.bass as bass
from concourse import mybir

F32 = mybir.dt.float32
F32R = mybir.dt.float32r
BF16 = mybir.dt.bfloat16
U32 = mybir.dt.uint32
ALU = mybir.AluOpType
ACT = mybir.ActivationFunctionType
AX = mybir.AxisListType

P = 128
B, DIMS, L, D = 16, 4, 256, 64
STEPS = 8
H, G, HG = 8, 2, 4
HD = 32
E = 8
TOK = B * L
CH = 512
NCH = TOK // CH
BPC = CH // L
NT = TOK // P
UW = L + 2
EPS = 1e-5
MASKED = -1e30
ONE_ROW = 32

W_COLS = {"wa": P, "w2": P, "wc": D, "w4": D}
C_COLS = {"ident": P, "wv": H * D, "w1": E * D, "sel": (E // 2) * P, "b2": P, "wo": 4 * D,
          "w2e": 4 * D, "wr": E, "b1": E // 2, "iota": E}


def places(widths):
    at, out = 0, {}
    for name, n in widths.items():
        out[name] = (at, at + n)
        at += n
    return out, at


W_AT, W_N = places(W_COLS)
C_AT, C_N = places(C_COLS)
A_MM, A_G, A_V, A_S = 12, 4, 2, 6
PT_W = L + P


def audio_tower(nc, xin, wtok, wqk, wconst, out):
    ctx = ExitStack()
    with ctx:
        def sb(name, shape, dt=F32):
            return ctx.enter_context(nc.sbuf_tensor(name, shape, dt))

        def sem(name):
            return ctx.enter_context(nc.semaphore(name))

        xrows = sb("xrows", [P, TOK])
        tok_w = sb("tok_w", [P, W_N])
        const_w = sb("const_w", [P, C_N])
        drive = sb("drive", [P, TOK])
        state = sb("state", [P, B, UW])
        presum = sb("presum", [P, 4, CH])
        qk_w = presum[0:D, 0:3, :].rearrange("p a b -> p (a b)")
        wg_high = sb("wg_high", [P, H, 2, D], F32R)
        wg_low = sb("wg_low", [P, H, 2, D], F32R)
        wv_high = sb("wv_high", [P, H * D], F32R)
        wv_low = sb("wv_low", [P, H * D], F32R)
        w1_high = sb("w1_high", [P, E * D], F32R)
        w1_low = sb("w1_low", [P, E * D], F32R)
        wr_high = sb("wr_high", [P, E], F32R)
        wr_low = sb("wr_low", [P, E], F32R)
        b2_high = sb("b2_high", [P, P], F32R)
        b2_low = sb("b2_low", [P, P], F32R)
        sel = sb("sel", [P, (E // 2) * P], F32R)
        ident_bf = sb("ident_bf", [P, P], BF16)
        causal_bf = sb("causal_bf", [P, 4, P], BF16)
        ones = sb("ones", [P, HD])
        half = sb("half", [P, 2])
        mixedT = sb("mixedT", [D, L])
        h1 = sb("h1", [P, NT, D])
        base = h1
        stat_n = sb("stat_n", [P, 2, 6])
        mom_n = sb("mom_n", [P, 2, 2])
        var_n = sb("var_n", [P, 2])
        rstd_n = sb("rstd_n", [P, 2])
        xn = sb("xn", [P, 2, D])
        rowx = [sb(f"rowx{q}", [P, 2, 2 * D + 2 * H], F32R) for q in range(2)]
        xs = [sb(f"xs{q}", [P, L], F32R) for q in range(2)]
        xz = sb("xz", [P, L], F32R)
        xm = sb("xm", [P, L], F32R)
        ga = [sb(f"ga{q}", [P, H, L], F32R) for q in range(2)]
        gb = [sb(f"gb{q}", [P, H, L], F32R) for q in range(2)]
        vals = [sb(f"vals{q}", [P, 2, H * D]) for q in range(2)]
        negmax = sb("negmax", [P, 2, H])
        pt = sb("pt", [P, H, PT_W])
        recip = sb("recip", [P, L])
        cxn = [sb(f"cxn{q}", [P, G, 2, L]) for q in range(2)]
        proj = sb("proj", [P, L])
        h2a = sb("h2a", [P, 2, D])
        h2 = sb("h2", [P, 2, D])
        stat_r = sb("stat_r", [P, 2, 6])
        mom_r = sb("mom_r", [P, 2, 2])
        var_r = sb("var_r", [P, 2])
        rstd_r = sb("rstd_r", [P, 2])
        yn = sb("yn", [P, 2, D])
        rowy = sb("rowy", [P, 2, 2 * D], F32R)
        ys = sb("ys", [P, L], F32R)
        ysall = sb("ysall", [P, TOK], F32R)
        srt = sb("srt", [P, 2, E])
        idx = sb("idx", [P, 2, E], U32)
        gap = sb("gap", [P, 2])
        egap = sb("egap", [P, 2])
        den = sb("den", [P, 2])
        wts = sb("wts", [P, 2, 2])
        hot = sb("hot", [P, 2, 2, E])
        hotw = sb("hotw", [P, 2, 2, E])
        comb = sb("comb", [P, 2, E])
        rowc = sb("rowc", [P, 2, 2 * E], F32R)
        combT = sb("combT", [P, TOK], F32R)
        hid = drive[:, 0:4 * CH].rearrange("p (t c) -> p t c", t=4)
        hidw = drive[:, 4 * CH:8 * CH].rearrange("p (t c) -> p t c", t=4)
        moe = presum[:, 0, :]
        outa = presum[:, 1, 0:CH // P * D].rearrange("p (t d) -> p t d", d=D)
        outb = presum[:, 2, 0:CH // P * D].rearrange("p (t d) -> p t d", d=D)

        def tw(name):
            a, z = W_AT[name]
            return tok_w[:, a:z]

        def cw(name):
            a, z = C_AT[name]
            return const_w[:, a:z]

        bank = [ctx.enter_context(nc.psum_tensor(f"bank{i}", [P, CH], F32)) for i in range(8)]
        key_bank = bank[0:2]
        prob_bank = bank[2:4]
        ctx_bank, sum_bank, norm_bank, rout_bank = bank[4:8]

        x_in, tok_in, qk_in, const_in = (sem(n) for n in ("x_in", "tok_in", "qk_in", "const_in"))
        zeroed, pool_consts, dve_consts, split_h, split_l = (sem(n) for n in ("zeroed", "pool_consts", "dve_consts", "split_h", "split_l"))
        pool_set = sem("pool_set")
        wg_mm, wg_h, wg_l = sem("wg_mm"), sem("wg_h"), sem("wg_l")
        drive_mm, drive_copied = sem("drive_mm"), sem("drive_copied")
        step_mm, step_sum, state_ready, down_ready, edge_zero = (
            sem(n) for n in ("step_mm", "step_sum", "state_ready", "down_ready", "edge_zero"))
        mixed_mm, mixed_relu, mixedT_mm, h1_copied = (sem(n) for n in ("mixed_mm", "mixed_relu", "mixedT_mm", "h1_copied"))
        n_stats, n_moms, n_var, n_rstd, n_xn, n_high, n_low = (
            sem(n) for n in ("n_stats", "n_moms", "n_var", "n_rstd", "n_xn", "n_high", "n_low"))
        xs_mm, xs_copied = sem("xs_mm"), sem("xs_copied")
        g_mm, g_high, g_low, v_mm, v_copied, s_mm, s_max, m_high, m_low = (
            sem(n) for n in ("g_mm", "g_high", "g_low", "v_mm", "v_copied", "s_mm", "s_max", "m_high", "m_low"))
        xm_mm, xm_copied, st_mm, st_exp, p_masked, pv_mm, sum_inv, ctx_normed = (
            sem(n) for n in ("xm_mm", "xm_copied", "st_mm", "st_exp", "p_masked", "pv_mm", "sum_inv", "ctx_normed"))
        o_mm, o_copied, oT_mm, r_h2a, r_h2, r_stats, r_moms, r_var, r_rstd, r_yn, r_high, r_low, r_base = (
            sem(n) for n in ("o_mm", "o_copied", "oT_mm", "r_h2a", "r_h2", "r_stats", "r_moms", "r_var", "r_rstd",
                             "r_yn", "r_high", "r_low", "r_base"))
        ys_mm, ys_copied, lg_mm, lg_sorted, lg_index, lg_gap, lg_exp, lg_den, lg_w0, lg_w1 = (
            sem(n) for n in ("ys_mm", "ys_copied", "lg_mm", "lg_sorted", "lg_index", "lg_gap", "lg_exp", "lg_den",
                             "lg_w0", "lg_w1"))
        c_hot, c_hotw, c_comb, c_high, c_low, c_mm, c_copied = (
            sem(n) for n in ("c_hot", "c_hotw", "c_comb", "c_high", "c_low", "c_mm", "c_copied"))
        up_mm, wt_mm, gelued, weighted, down_mm, moe_copied, moeT_mm, out_a, out_b, out_dma = (
            sem(n) for n in ("up_mm", "wt_mm", "gelued", "weighted", "down_mm", "moe_copied", "moeT_mm", "out_a",
                             "out_b", "out_dma"))

        def after(eng, signal, count, apart=False):
            if isinstance(count, int):
                if count > 0:
                    eng.wait_ge(signal, count)
                return
            if apart:
                count = eng.to_reg(count)
                eng.wait_ge(signal, 1)
            eng.wait_ge(signal, count)

        def pipeline(eng, step):
            def peeled(s):
                step(s, s % 2, [0 <= s - back < B for back in range(5)])
            for s in range(6):
                peeled(s)
            with eng.Fori(3, B // 2) as i:
                for q in range(2):
                    step(2 * i + q, q, [True] * 5)
            for s in range(B, B + 4):
                peeled(s)

        def chunks(eng, chunk):
            chunk(0)
            with eng.Fori(1, NCH) as k:
                chunk(k)
            chunk(NCH)

        seq2 = lambda c: slice(BPC * c, BPC * c + BPC)
        two = lambda ap: ap.rearrange("p (b l) -> p b l", b=BPC)

        block = ctx.enter_context(nc.Block())

        @block.sync
        def _(sp):
            sp.dma_start(tok_w[:, :], wtok).then_inc(tok_in, 16)
            sp.wait_ge(zeroed, 1)
            sp.dma_start(xrows[0:2 * DIMS, :], xin).then_inc(x_in, 16)
            sp.dma_start(qk_w, wqk).then_inc(qk_in, 16)
            sp.dma_start(const_w[:, :], wconst).then_inc(const_in, 16)

            def chunk(k):
                if isinstance(k, int) and k == 0:
                    return
                sp.wait_ge(out_b, k)
                sp.dma_start(out[bass.ds((k - 1) * CH, CH), :].rearrange("(t p) d -> p t d", p=P),
                             outb).then_inc(out_dma, 16)
            chunks(sp, chunk)
            sp.wait_ge(out_dma, 16 * NCH)

        @block.gpsimd
        def _(pool):
            g = nc.gpsimd
            g.memset(causal_bf[:, :, :], 0.0).then_inc(pool_set, 1)
            for q in range(2):
                g.memset(gb[q][:, :, :].bitcast(F32), 0.0).then_inc(pool_set, 1)
            g.memset(half[:, :], -0.5).then_inc(pool_consts, 1)
            g.memset(ones[:, :], 1.0).then_inc(pool_consts, 1)
            pool.wait_ge(pool_set, 3)
            g.affine_select(out=causal_bf[:, :, :], in_=causal_bf[:, :, :], compare_op=ALU.is_ge, fill=MASKED,
                            base=0, pattern=[[0, 4], [-1, P]], channel_multiplier=1).then_inc(pool_consts, 1)
            for part in range(2):
                if part:
                    pool.wait_ge(pool_set, 5)
                for q in range(2):
                    last = g.affine_select(out=gb[q][:, :, :], in_=gb[q][:, :, :], compare_op=ALU.not_equal,
                                           fill=1.0, base=-D - H * part, pattern=[[-1, H], [0, L]],
                                           channel_multiplier=1)
                    last.then_inc(pool_consts if part else pool_set, 1)
            pool.wait_ge(const_in, 16)
            for high, low, w in ((wv_high, wv_low, "wv"), (wr_high, wr_low, "wr"), (w1_high, w1_low, "w1"),
                                 (b2_high, b2_low, "b2"), (sel, None, "sel")):
                g.tensor_copy(high[:, :], cw(w)).then_inc(split_h, 1)
            for n, (high, low, w) in enumerate(((wv_high, wv_low, "wv"), (wr_high, wr_low, "wr"),
                                                (w1_high, w1_low, "w1"), (b2_high, b2_low, "b2"))):
                pool.wait_ge(split_h, n + 1)
                g.tensor_tensor(low[:, :], cw(w), high[:, :].bitcast(F32), ALU.subtract).then_inc(split_l, 1)
            pool.wait_ge(pool_consts, 2)

            def rstd(b, moms, mom, var, s_var, rs, s_rstd):
                after(pool, moms, 2 * b + 2, apart=True)
                g.tensor_scalar(var[:, :], mom[:, :, 1], 1.0, EPS, ALU.mult, ALU.add).then_inc(s_var, 1)
                after(pool, s_var, b + 1)
                g.tensor_tensor(rs[:, :], var[:, :], half[:, :], ALU.pow).then_inc(s_rstd, 1)

            def mask_diagonal(b, grp, kb):
                after(pool, st_exp, 6 * b + 3 * grp + 2 + kb, apart=True)
                v = pt[:, HG * grp:HG * grp + HG, L * kb:L * kb + P]
                g.affine_select(out=v, in_=v, compare_op=ALU.is_ge, fill=0.0, base=0,
                                pattern=[[0, HG], [1, P]], channel_multiplier=-1).then_inc(p_masked, 1)

            def step(s, q, on):
                if on[4]:
                    b = s - 4
                    after(pool, c_hot, b + 1)
                    after(pool, lg_w1, b + 1)
                    g.tensor_tensor(hotw[:, :, :, :], hot[:, :, :, :],
                                    wts[:, :, :].unsqueeze(3).broadcast_to([P, 2, 2, E]),
                                    ALU.mult).then_inc(c_hotw, 1)
                    after(pool, c_hotw, b + 1)
                    after(pool, c_mm, b)
                    g.tensor_tensor(comb[:, :, :], hotw[:, :, 0, :], hotw[:, :, 1, :], ALU.add).then_inc(c_comb, 1)
                    after(pool, c_comb, b + 1, apart=True)
                    g.tensor_copy(rowc[:, :, 0:E], comb[:, :, :]).then_inc(c_high, 1)
                    after(pool, c_high, b + 1)
                    g.tensor_tensor(rowc[:, :, E:2 * E], comb[:, :, :], rowc[:, :, 0:E].bitcast(F32),
                                    ALU.subtract).then_inc(c_low, 1)
                if on[2]:
                    mask_diagonal(s - 2, 0, 0)
                if on[3]:
                    rstd(s - 3, r_moms, mom_r, var_r, r_var, rstd_r, r_rstd)
                if on[2]:
                    mask_diagonal(s - 2, 0, 1)
                if on[0]:
                    rstd(s, n_moms, mom_n, var_n, n_var, rstd_n, n_rstd)
                if on[3]:
                    b = s - 3
                    after(pool, r_yn, 2 * b + 2)
                    g.tensor_tensor(base[:, bass.ds(2 * b, 2), :], h2[:, :, :], yn[:, :, :],
                                    ALU.add).then_inc(r_base, 1)
                if on[2]:
                    mask_diagonal(s - 2, 1, 0)
                    mask_diagonal(s - 2, 1, 1)

            pipeline(pool, step)

        @block.scalar
        def _(act):
            a = nc.scalar
            act.wait_ge(wg_mm, 1)
            for r in range(2):
                a.activation(wg_high[:, :, r, :], bank[7][:, :].rearrange("p (h d) -> p h d", h=H),
                             ACT.Copy).then_inc(wg_h, 1)
            for c in range(NCH):
                act.wait_ge(drive_copied, c + 1)
                a.activation(state[:, seq2(c), 1:1 + L], two(bank[c][:, :]), ACT.Relu).then_inc(state_ready, 1)
            with act.Fori(0, STEPS - 2) as t:
                for c in range(NCH):
                    act.wait_ge(step_sum, NCH * t + c + 1)
                    a.activation(state[:, seq2(c), 1:1 + L], two(presum[:, c % 4, :]), ACT.Relu).then_inc(state_ready, 1)
            for c in range(NCH):
                act.wait_ge(step_sum, NCH * (STEPS - 2) + c + 1)
                a.activation(state[0:D, seq2(c), 1:1 + L], two(presum[0:D, c % 4, :]), ACT.Relu).then_inc(state_ready, 1)

            def g_high_part(b, q, t):
                after(act, g_mm, A_G * b + t + 1)
                a.activation(ga[q][:, 2 * t:2 * t + 2, :], key_bank[t % 2][:, :].rearrange("p (h l) -> p h l", h=2),
                             ACT.Copy).then_inc(g_high, 1)

            def exp_scores(b, t):
                after(act, st_mm, 6 * b + t + 1)
                grp, part = t // 3, t % 3
                src = prob_bank[t % 2][:, :]
                if part < 2:
                    n = HG * grp + 2 * part
                    a.activation(pt[:, n:n + 2, 0:L], src.rearrange("p (h l) -> p h l", h=2), ACT.Exp).then_inc(st_exp, 1)
                else:
                    a.activation(pt[:, HG * grp:HG * grp + HG, L:PT_W], src.rearrange("p (h l) -> p h l", h=HG),
                                 ACT.Exp).then_inc(st_exp, 1)

            def step(s, q, on):
                r = 1 - q
                if on[4]:
                    b = s - 4
                    after(act, lg_gap, b + 1)
                    a.activation(egap[:, :], gap[:, :], ACT.Exp).then_inc(lg_exp, 1)
                if on[2]:
                    b = s - 2
                    after(act, xm_mm, b + 1)
                    a.activation(xm[0:D + 2 * H, :], norm_bank[0:D + 2 * H, 0:L], ACT.Copy).then_inc(xm_copied, 1)
                if on[3]:
                    b = s - 3
                    after(act, o_mm, b + 1)
                    after(act, oT_mm, b)
                    a.activation(proj[:, :], rout_bank[:, 0:L], ACT.Copy).then_inc(o_copied, 1)
                if on[1]:
                    g_high_part(s - 1, r, 0)
                    g_high_part(s - 1, r, 1)
                if on[0]:
                    after(act, mixed_mm, s + 1)
                    a.activation(mixedT[:, :], norm_bank[0:D, 0:L], ACT.Relu).then_inc(mixed_relu, 1)
                if on[2]:
                    exp_scores(s - 2, 0)
                if on[1]:
                    g_high_part(s - 1, r, 2)
                if on[2]:
                    exp_scores(s - 2, 1)
                if on[1]:
                    g_high_part(s - 1, r, 3)
                if on[2]:
                    exp_scores(s - 2, 2)
                if on[1]:
                    for t in range(A_V):
                        after(act, v_mm, A_V * (s - 1) + t + 1)
                        a.activation(vals[r][:, t, :], key_bank[t % 2][:, :], ACT.Copy).then_inc(v_copied, 1)
                if on[0]:
                    after(act, mixedT_mm, s + 1)
                    a.activation(h1[:, bass.ds(2 * s, 2), :],
                                 norm_bank[:, 0:2 * D].rearrange("p (t d) -> p t d", t=2), ACT.Copy).then_inc(h1_copied, 1)
                if on[2]:
                    for t in (3, 4, 5):
                        exp_scores(s - 2, t)
                if on[4]:
                    b = s - 4
                    after(act, c_mm, b + 1)
                    a.activation(combT[0:2 * E, bass.ds(L * b, L)], rout_bank[0:2 * E, 0:L], ACT.Copy).then_inc(c_copied, 1)
                if on[3]:
                    b = s - 3
                    after(act, ys_mm, b + 1)
                    a.activation(ys[:, :], rout_bank[:, 0:L], ACT.Copy).then_inc(ys_copied, 1)
                    a.activation(ysall[:, bass.ds(L * b, L)], rout_bank[:, 0:L], ACT.Copy).then_inc(ys_copied, 1)
                if on[0]:
                    after(act, xs_mm, s + 1)
                    a.activation(xs[q][:, :], norm_bank[:, 0:L], ACT.Copy).then_inc(xs_copied, 1)
                    a.activation(xz[0:D, :], norm_bank[D:P, 0:L], ACT.Copy).then_inc(xs_copied, 1)

            pipeline(act, step)

            def chunk(k):
                if isinstance(k, int) and k == NCH:
                    act.wait_ge(down_mm, k)
                    act.wait_ge(moeT_mm, k - 1)
                    a.activation(moe, bank[4][:, :], ACT.Copy).then_inc(moe_copied, 1)
                    return
                for p in range(4):
                    after(act, up_mm, 4 * k + p + 1)
                    after(act, weighted, 4 * (k - 1) + p + 1)
                    a.activation(hid[:, p, :], bank[p % 2][:, :], ACT.Gelu, bias=cw("b1")[:, p:p + 1]).then_inc(gelued, 1)
                    if p == 1 and not (isinstance(k, int) and k == 0):
                        after(act, down_mm, k)
                        after(act, moeT_mm, k - 1)
                        a.activation(moe, bank[4][:, :], ACT.Copy).then_inc(moe_copied, 1)
            chunks(act, chunk)

        @block.vector
        def _(dve):
            v = nc.vector
            v.memset(xrows[:, :], 0.0).then_inc(edge_zero, 1)
            dve.wait_ge(edge_zero, 1)
            v.memset(xrows[ONE_ROW:2 * ONE_ROW, :], 1.0).then_inc(zeroed, 1)
            v.memset(state[:, :, 0:1], 0.0).then_inc(edge_zero, 1)
            v.memset(xz[D:P, :].bitcast(F32), 0.0).then_inc(dve_consts, 1)
            v.memset(xm[D:P, :].bitcast(F32), 0.0).then_inc(dve_consts, 1)
            dve.wait_ge(wg_h, 2)
            for r in range(2):
                v.tensor_tensor(wg_low[:, :, r, :], bank[7][:, :].rearrange("p (h d) -> p h d", h=H),
                                wg_high[:, :, r, :].bitcast(F32), ALU.subtract).then_inc(wg_l, 1)
            for c in range(NCH):
                dve.wait_ge(drive_mm, c + 1)
                v.tensor_copy(drive[:, CH * c:CH * c + CH], bank[c][:, :]).then_inc(drive_copied, 1)
            v.memset(combT[:, :].bitcast(F32), 0.0).then_inc(dve_consts, 1)
            dve.wait_ge(const_in, 16)
            v.tensor_copy(ident_bf[:, :], cw("ident")).then_inc(dve_consts, 1)

            def step_presum(t, c):
                dve.wait_ge(step_mm, NCH * t + c + 1)
                dve.wait_ge(state_ready, NCH * t + c + 5)
                v.tensor_tensor(presum[:, c % 4, :], bank[c][:, :], drive[:, CH * c:CH * c + CH], ALU.add).then_inc(step_sum, 1)

            with dve.Fori(0, STEPS - 2) as t:
                for c in range(NCH):
                    step_presum(t, c)
            t = STEPS - 2
            for c in range(NCH):
                if c >= 4:
                    dve.wait_ge(down_ready, c - 3)
                step_presum(t, c)
                dve.wait_ge(step_sum, NCH * t + c + 1)
                v.tensor_scalar(state[D:P, seq2(c), L - 2::-1], two(presum[D:P, c % 4, :])[:, :, 0:L - 1], 0.0, None,
                                ALU.max).then_inc(down_ready, 1)
            v.memset(state[D:P, :, L - 1:L], 0.0).then_inc(down_ready, 1)

            def g_low_part(b, q, t):
                after(dve, g_high, A_G * b + t + 1)
                v.tensor_tensor(gb[q][0:D, 2 * t:2 * t + 2, :],
                                key_bank[t % 2][0:D, :].rearrange("p (h l) -> p h l", h=2),
                                ga[q][0:D, 2 * t:2 * t + 2, :].bitcast(F32), ALU.subtract).then_inc(g_low, 1)

            def score_max(b, t):
                after(dve, s_mm, A_S * b + t + 1)
                if t == 0:
                    after(dve, m_low, b)
                if t < 2:
                    o, src = negmax[:, 0, 4 * t:4 * t + 4], key_bank[t % 2][:, :].rearrange("p (h l) -> p h l", h=4)
                else:
                    o = negmax[:, 1, 2 * (t - 2):2 * (t - 2) + 2]
                    src = key_bank[t % 2][:, :].rearrange("p (h l) -> p h l", h=2)
                v.tensor_reduce(o, src, AX.X, ALU.max, negate=True).then_inc(s_max, 1)

            def moments(b, src, stat, s_stats, mom, s_moms):
                for t in range(2):
                    v.bn_stats(stat[:, t, :], src(t)).then_inc(s_stats, 1)
                for t in range(2):
                    after(dve, s_stats, 2 * b + t + 1, apart=True)
                    v.bn_aggr(mom[:, t, :], stat[:, t, :]).then_inc(s_moms, 1)

            def normed(b, src, mom, s_rstd, rs, o, s_o):
                after(dve, s_rstd, b + 1)
                for t in range(2):
                    v.tensor_scalar(o[:, t, :], src(t), mom[:, t, 0:1], rs[:, t:t + 1], ALU.subtract,
                                    ALU.mult).then_inc(s_o, 1)
                after(dve, s_o, 2 * b + 2)

            def context(b, q, grp):
                after(dve, pv_mm, 2 * b + grp + 1)
                after(dve, ctx_normed, 2 * b + grp)
                v.reciprocal(recip[:, :], sum_bank[:, 0:L]).then_inc(sum_inv, 1)
                after(dve, sum_inv, 2 * b + grp + 1)
                v.tensor_tensor(cxn[q][:, grp, :, :], ctx_bank[:, :].rearrange("p (h l) -> p h l", h=2),
                                recip[:, :].unsqueeze(1).broadcast_to([P, 2, L]), ALU.mult).then_inc(ctx_normed, 1)

            def step(s, q, on):
                r = 1 - q
                if on[4]:
                    b = s - 4
                    after(dve, lg_exp, b + 1)
                    v.tensor_scalar(den[:, :], egap[:, :], 1.0, None, ALU.add).then_inc(lg_den, 1)
                    after(dve, lg_den, b + 1)
                    v.reciprocal(wts[:, :, 0], den[:, :]).then_inc(lg_w0, 1)
                    after(dve, lg_w0, b + 1)
                    v.tensor_tensor(wts[:, :, 1], egap[:, :], wts[:, :, 0], ALU.mult).then_inc(lg_w1, 1)
                if on[1]:
                    for t in range(A_G):
                        g_low_part(s - 1, r, t)
                if on[3]:
                    b = s - 3
                    src = rout_bank[:, 0:2 * P].rearrange("p (t e) -> p t e", t=2)
                    after(dve, oT_mm, b + 1)
                    v.tensor_tensor(h2a[:, :, :], src[:, :, 0:D], h1[:, bass.ds(2 * b, 2), :], ALU.add).then_inc(r_h2a, 1)
                    after(dve, r_h2a, b + 1)
                    after(dve, r_base, b)
                    v.tensor_tensor(h2[:, :, :], src[:, :, D:P], h2a[:, :, :], ALU.add).then_inc(r_h2, 1)
                    after(dve, r_h2, b + 1)
                    moments(b, lambda t: h2[:, t, :], stat_r, r_stats, mom_r, r_moms)
                if on[1]:
                    score_max(s - 1, 0)
                if on[0]:
                    after(dve, h1_copied, s + 1)
                    moments(s, lambda t: h1[:, bass.ds(2 * s + t, 1), :].rearrange("p o d -> p (o d)"), stat_n,
                            n_stats, mom_n, n_moms)
                if on[1]:
                    score_max(s - 1, 1)
                if on[3]:
                    b = s - 3
                    normed(b, lambda t: h2[:, t, :], mom_r, r_rstd, rstd_r, yn, r_yn)
                    v.tensor_copy(rowy[:, :, D:2 * D], yn[:, :, :]).then_inc(r_high, 1)
                    after(dve, r_high, b + 1)
                    v.tensor_tensor(rowy[:, :, 0:D], yn[:, :, :], rowy[:, :, D:2 * D].bitcast(F32),
                                    ALU.subtract).then_inc(r_low, 1)
                if on[0]:
                    normed(s, lambda t: h1[:, bass.ds(2 * s + t, 1), :].rearrange("p o d -> p (o d)"), mom_n, n_rstd,
                           rstd_n, xn, n_xn)
                    v.tensor_copy(rowx[q][:, :, D:2 * D], xn[:, :, :]).then_inc(n_high, 1)
                    after(dve, n_high, s + 1)
                    v.tensor_tensor(rowx[q][:, :, 0:D], xn[:, :, :], rowx[q][:, :, D:2 * D].bitcast(F32),
                                    ALU.subtract).then_inc(n_low, 1)
                if on[2]:
                    context(s - 2, q, 0)
                if on[1]:
                    score_max(s - 1, 2)
                    score_max(s - 1, 3)
                if on[2]:
                    context(s - 2, q, 1)
                if on[1]:
                    b = s - 1
                    score_max(b, 4)
                    score_max(b, 5)
                    after(dve, s_max, A_S * b + A_S)
                    v.tensor_copy(rowx[r][:, :, 2 * D:2 * D + H], negmax[:, :, :]).then_inc(m_high, 1)
                    after(dve, m_high, b + 1)
                    v.tensor_tensor(rowx[r][:, :, 2 * D + H:2 * D + 2 * H], negmax[:, :, :],
                                    rowx[r][:, :, 2 * D:2 * D + H].bitcast(F32), ALU.subtract).then_inc(m_low, 1)
                if on[3]:
                    b = s - 3
                    after(dve, lg_mm, b + 1, apart=True)
                    for t in range(2):
                        v.max(srt[:, t, :], rout_bank[:, E * t:E * t + E]).then_inc(lg_sorted, 1)
                    for t in range(2):
                        after(dve, lg_sorted, 2 * b + t + 1, apart=True)
                        v.max_index(idx[:, t, :], srt[:, t, :], rout_bank[:, E * t:E * t + E]).then_inc(lg_index, 1)
                    after(dve, lg_index, 2 * b + 2)
                    after(dve, c_hotw, b)
                    v.tensor_tensor(hot[:, :, :, :], cw("iota").unsqueeze(1).unsqueeze(1).broadcast_to([P, 2, 2, E]),
                                    idx[:, :, 0:2].unsqueeze(3).broadcast_to([P, 2, 2, E]),
                                    ALU.is_equal).then_inc(c_hot, 1)
                    after(dve, lg_exp, b)
                    v.tensor_tensor(gap[:, :], srt[:, :, 1], srt[:, :, 0], ALU.subtract).then_inc(lg_gap, 1)

            pipeline(dve, step)

            def chunk(k):
                first = isinstance(k, int) and k == 0
                last = isinstance(k, int) and k == NCH

                def leave():
                    src = bank[5][:, :].rearrange("p (t e) -> p t e", t=CH // P)
                    after(dve, moeT_mm, k)
                    v.tensor_tensor(outa, src[:, :, 0:D], base[:, bass.ds((k - 1) * (CH // P), CH // P), :],
                                    ALU.add).then_inc(out_a, 1)
                    after(dve, out_a, k)
                    after(dve, out_dma, 16 * (k - 1))
                    v.tensor_tensor(outb, src[:, :, D:P], outa, ALU.add).then_inc(out_b, 1)
                if last:
                    leave()
                    return
                for p in range(4):
                    after(dve, gelued, 4 * k + p + 1)
                    after(dve, wt_mm, 4 * k + p + 1)
                    after(dve, down_mm, k)
                    v.tensor_tensor(hidw[:, p, :], bank[2 + p % 2][:, :], hid[:, p, :], ALU.mult).then_inc(weighted, 1)
                    if p == 3 and not first:
                        leave()
            chunks(dve, chunk)

        @block.tensor
        def _(pe):
            mm = nc.tensor.matmul
            ident = cw("ident")

            def tr(o, src):
                return nc.tensor.transpose(o, src.bitcast(F32), ident[0:src.shape[0], 0:src.shape[0]])

            pe.wait_ge(qk_in, 16)
            qT = qk_w[:, 0:H * 2 * D].rearrange("p (h e) -> p h e", h=H)
            kT = qk_w[:, H * 2 * D:H * 3 * D].rearrange("p (h e) -> p h e", h=H)
            for n in range(H):
                last = mm(bank[7][:, n * D:n * D + D], qT[:, n, :], kT[:, n, :], start=True, stop=True)
            last.then_inc(wg_mm, 1)
            pe.wait_ge(tok_in, 16)
            pe.wait_ge(x_in, 16)
            for c in range(NCH):
                if c == 7:
                    pe.wait_ge(wg_l, 2)
                mm(bank[c][:, :], tw("wa"), xrows[:, CH * c:CH * c + CH], start=True, stop=True).then_inc(drive_mm, 1)
            pe.wait_ge(edge_zero, 2)
            with pe.Fori(0, STEPS - 1) as t:
                for c in range(NCH):
                    pe.wait_ge(state_ready, NCH * t + c + 1)
                    mm(bank[c][:, :], tw("w2"), state[:, seq2(c), 0:L], start=True, stop=True).then_inc(step_mm, 1)
            pe.wait_ge(state_ready, NCH * STEPS)
            pe.wait_ge(down_ready, NCH + 1)
            pe.wait_ge(pool_consts, 5)
            pe.wait_ge(dve_consts, 4)
            pe.wait_ge(split_h, 5)
            pe.wait_ge(split_l, 4)

            def g_product(b, q, t):
                after(pe, s_max if t < 2 else g_low, A_S * (b - 1) + 5 + t if t < 2 else A_G * b + t - 1)
                for n in (2 * t, 2 * t + 1):
                    o = key_bank[t % 2][:, L * (n % 2):L * (n % 2) + L]
                    mm(o, wg_high[:, n, :, :], xs[q][:, :], start=True, stop=False)
                    last = mm(o, wg_low[:, n, :, :], xs[q][:, :], start=False, stop=True)
                last.then_inc(g_mm, 1)

            def v_product(b, q, t):
                after(pe, g_low, A_G * b + 3 + t)
                mm(key_bank[t % 2][:, :], xs[q][:, P * t:P * t + P], wv_high[:, :], start=True, stop=False)
                mm(key_bank[t % 2][:, :], xs[q][:, P * t:P * t + P], wv_low[:, :], start=False,
                   stop=True).then_inc(v_mm, 1)

            def score_product(b, q, t):
                after(pe, v_copied if t < 2 else s_max, A_V * b + t + 1 if t < 2 else A_S * b + t - 1)
                jb = 0 if t < 2 else 1
                heads = slice(4 * t, 4 * t + 4) if t < 2 else slice(2 * (t - 2), 2 * (t - 2) + 2)
                nk = P if t < 2 else L
                nh = CH // nk
                o = key_bank[t % 2][:, :].rearrange("p (h l) -> p h l", h=nh)
                mm(o, xs[q][:, P * jb:P * jb + P], ga[q][:, heads, 0:nk], start=True, stop=False)
                mm(o, xz[:, P * jb:P * jb + P], gb[q][:, heads, 0:nk], start=False, stop=False)
                mm(o[:, :, nk - P:nk], ident_bf[:, :], causal_bf[:, 0:nh, :], start=False, stop=True).then_inc(s_mm, 1)

            def prob_product(b, q, t):
                if t < 2:
                    after(pe, st_exp, 6 * b + t - 1)
                    after(pe, xm_copied, b + 1)
                else:
                    after(pe, st_exp, 6 * b + t - 1)
                grp, part = t // 3, t % 3
                for i in range(2 if part < 2 else 4):
                    n = HG * grp + (2 * part + i if part < 2 else i)
                    w = L if part < 2 else P
                    keys = slice(0, P) if part < 2 else slice(P, L)
                    o = prob_bank[t % 2][:, w * i:w * i + w]
                    mm(o, ga[q][:, n, keys], xs[q][:, L - w:L], start=True, stop=False)
                    last = mm(o, gb[q][:, n, keys], xm[:, L - w:L], start=False, stop=True)
                last.then_inc(st_mm, 1)

            def context_product(b, q, grp):
                after(pe, p_masked, 4 * b + 2 * grp + 2)
                after(pe, ctx_normed, 2 * b + grp)
                for hf in range(3):
                    for kb in range(2):
                        for c in range(HG):
                            n = HG * grp + c
                            rows = slice(HD * c, HD * c + HD)
                            o = ctx_bank[rows, L * hf:L * hf + L] if hf < 2 else sum_bank[rows, 0:L]
                            w = vals[q][:, kb, n * D + HD * hf:n * D + HD * hf + HD] if hf < 2 else ones[:, :]
                            last = mm(o[:, P * kb:L], w, pt[:, n, L * kb:L * kb + L - P * kb], start=(kb == 0),
                                      stop=(kb == 1))
                last.then_inc(pv_mm, 1)

            def step(s, q, on):
                r = 1 - q
                if on[2]:
                    b = s - 2
                    after(pe, m_low, b + 1)
                    after(pe, xs_copied, 2 * (b + 2) if on[0] else 2 * B)
                    for t in range(2):
                        last = tr(norm_bank[0:D + 2 * H, P * t:P * t + P], rowx[q][:, t, D:2 * D + 2 * H])
                    last.then_inc(xm_mm, 1)
                if on[3]:
                    b = s - 3
                    after(pe, ctx_normed, 2 * b + 2)
                    after(pe, lg_index, 2 * b)
                    for grp in range(G):
                        for hf in range(2):
                            last = mm(rout_bank[D * grp:D * grp + D, 0:L],
                                      cw("wo")[:, D * (2 * grp + hf):D * (2 * grp + hf) + D],
                                      cxn[r][:, grp, hf, :], start=(hf == 0), stop=(hf == 1))
                    last.then_inc(o_mm, 1)
                if on[1]:
                    after(pe, xs_copied, 2 * s)
                    g_product(s - 1, r, 0)
                    g_product(s - 1, r, 1)
                if on[0]:
                    after(pe, xm_copied, s - 1)
                    after(pe, xs_copied, 2 * s)
                    o = norm_bank[0:D, 0:L]
                    mm(o, tw("wc"), xrows[:, bass.ds(L * s, L)], start=True, stop=False)
                    mm(o, tw("w4"), state[:, bass.ds(s, 1), 0:L].rearrange("p o l -> p (o l)"), start=False,
                       stop=True).then_inc(mixed_mm, 1)
                if on[2]:
                    prob_product(s - 2, q, 0)
                if on[1]:
                    g_product(s - 1, r, 2)
                if on[2]:
                    prob_product(s - 2, q, 1)
                if on[1]:
                    g_product(s - 1, r, 3)
                if on[2]:
                    prob_product(s - 2, q, 2)
                if on[3]:
                    after(pe, o_copied, s - 2)
                    for t in range(2):
                        last = tr(rout_bank[:, P * t:P * t + P], proj[:, P * t:P * t + P])
                    last.then_inc(oT_mm, 1)
                if on[1]:
                    v_product(s - 1, r, 0)
                    v_product(s - 1, r, 1)
                if on[0]:
                    after(pe, mixed_relu, s + 1, apart=True)
                    for t in range(2):
                        last = tr(norm_bank[:, D * t:D * t + D], mixedT[:, P * t:P * t + P])
                    last.then_inc(mixedT_mm, 1)
                if on[2]:
                    prob_product(s - 2, q, 3)
                if on[1]:
                    score_product(s - 1, r, 0)
                if on[2]:
                    prob_product(s - 2, q, 4)
                if on[1]:
                    score_product(s - 1, r, 1)
                if on[2]:
                    prob_product(s - 2, q, 5)
                if on[4]:
                    b = s - 4
                    after(pe, c_low, b + 1)
                    after(pe, r_h2 if on[3] else lg_index, b + 2 if on[3] else 2 * B)
                    for t in range(2):
                        last = tr(rout_bank[0:2 * E, P * t:P * t + P], rowc[:, t, :])
                    last.then_inc(c_mm, 1)
                if on[2]:
                    context_product(s - 2, q, 0)
                if on[1]:
                    score_product(s - 1, r, 2)
                    score_product(s - 1, r, 3)
                if on[3]:
                    b = s - 3
                    after(pe, r_low, b + 1)
                    after(pe, c_copied, b)
                    for t in range(2):
                        last = tr(rout_bank[:, P * t:P * t + P], rowy[:, t, :])
                    last.then_inc(ys_mm, 1)
                if on[2]:
                    context_product(s - 2, q, 1)
                if on[1]:
                    score_product(s - 1, r, 4)
                    score_product(s - 1, r, 5)
                if on[0]:
                    after(pe, n_low, s + 1)
                    for t in range(2):
                        last = tr(norm_bank[:, P * t:P * t + P], rowx[q][:, t, 0:2 * D])
                    last.then_inc(xs_mm, 1)
                if on[3]:
                    b = s - 3
                    after(pe, ys_copied, 2 * b + 2)
                    for t in range(2):
                        o = rout_bank[:, E * t:E * t + E]
                        mm(o, ys[:, P * t:P * t + P], wr_high[:, :], start=True, stop=False)
                        last = mm(o, ys[:, P * t:P * t + P], wr_low[:, :], start=False, stop=True)
                    last.then_inc(lg_mm, 1)

            pipeline(pe, step)

            pe.wait_ge(c_copied, B)
            pe.wait_ge(s_max, A_S * B)
            pe.wait_ge(st_exp, 6 * B)
            pe.wait_ge(ctx_normed, 2 * B)

            def up(k, p):
                after(pe, gelued, 4 * k + p - 1)
                cols = bass.ds(CH * k, CH)
                mm(bank[p % 2][:, :], w1_high[:, P * p:P * p + P], ysall[:, cols], start=True, stop=False)
                mm(bank[p % 2][:, :], w1_low[:, P * p:P * p + P], ysall[:, cols], start=False,
                   stop=True).then_inc(up_mm, 1)
                after(pe, weighted, 4 * k + p - 1)
                mm(bank[2 + p % 2][:, :], sel[:, P * p:P * p + P], combT[:, cols], start=True, stop=True).then_inc(wt_mm, 1)

            def down(k, p):
                if p == 0:
                    after(pe, moe_copied, k)
                    cols = bass.ds(CH * k, CH)
                    mm(bank[4][:, :], b2_high[:, :], combT[:, cols], start=True, stop=False)
                    mm(bank[4][:, :], b2_low[:, :], combT[:, cols], start=False, stop=False)
                half_rows = slice(D * (p // 2), D * (p // 2) + D)
                after(pe, weighted, 4 * k + p + 1)
                last = mm(bank[4][half_rows, :], cw("w2e")[:, D * p:D * p + D], hidw[:, p, :], start=False,
                          stop=(p % 2 == 1))
                if p == 3:
                    last.then_inc(down_mm, 1)

            def turn(k):
                after(pe, moe_copied, k)
                after(pe, out_b, k - 1)
                for t in range(CH // P):
                    last = tr(bank[5][:, P * t:P * t + P], moe[:, P * t:P * t + P])
                last.then_inc(moeT_mm, 1)

            def chunk(k):
                first = isinstance(k, int) and k == 0
                if isinstance(k, int) and k == NCH:
                    down(k - 1, 2)
                    down(k - 1, 3)
                    turn(k)
                    return
                for p in range(4):
                    up(k, p)
                    if p < 2 and not first:
                        down(k - 1, p + 2)
                    if p == 3 and not first:
                        turn(k)
                    if p >= 2:
                        down(k, p - 2)
            chunks(pe, chunk)


def kernel(**inputs):
    import concourse.bacc as bacc
    from concourse.bass_utils import run_bass_kernel_spmd

    f = {k: np.asarray(v) for k, v in inputs.items()}
    z = lambda *shape: np.zeros(shape, np.float32)
    x = f["x"].transpose(1, 0, 2)
    xin = np.concatenate([x, x[:, :, ::-1]], 0).reshape(2 * DIMS, TOK)

    wa = z(P, P)
    wa[0:DIMS, 0:D] = wa[DIMS:2 * DIMS, D:P] = f["L0_tok_W1"].T
    for i, name in enumerate(("L0_tok_b1", "L0_tok_b2")):
        wa[ONE_ROW + i] = np.concatenate([f[name], f[name]])
    w2 = z(P, P)
    w2[0:D, 0:D] = w2[D:P, D:P] = f["L0_tok_W2"].T
    wc = z(P, D)
    wc[0:DIMS] = f["L0_tok_W3"].T
    for i, name in enumerate(("L0_tok_b3", "L0_tok_b4", "L0_tok_b4")):
        wc[ONE_ROW + i] = f[name]
    w4 = np.concatenate([f["L0_tok_W4"].T] * 2, 0)
    wtok = np.concatenate([wa, w2, wc, w4], 1)

    q = f["L0_attn_query_matrices"].transpose(2, 0, 1)
    k = f["L0_attn_key_matrices"].transpose(2, 0, 1)
    wqk = np.concatenate([np.concatenate([q, q], 2).reshape(D, H * 2 * D), k.reshape(D, H * D)], 1)

    double = lambda a: np.concatenate([a, a], 0)
    wv = double(f["L0_attn_value_in_matrices"].transpose(1, 0, 2).reshape(D, H * D))
    w1 = double(f["L0_ffn_w1"].transpose(1, 0, 2).reshape(D, E * D))
    wr = double(f["L0_ffn_router_w"].T)
    sel = z(P, E // 2, 2, D)
    for e in range(E):
        sel[e, e // 2, e % 2] = sel[E + e, e // 2, e % 2] = 1.0
    b2 = z(P, P)
    b2[0:E, 0:D] = b2[E:2 * E, 0:D] = f["L0_ffn_b2"]
    wo = f["L0_attn_value_out_matrices"].reshape(G, HG, 2, HD, D).transpose(1, 3, 0, 2, 4).reshape(P, 4 * D)
    w2e = f["L0_ffn_w2"].reshape(E // 2, P, D).transpose(1, 0, 2).reshape(P, 4 * D)
    b1 = f["L0_ffn_b1"].reshape(E // 2, P).T
    iota = np.tile(np.arange(E, dtype=np.float32), (P, 1))
    parts = {"ident": np.eye(P, dtype=np.float32), "wv": wv, "w1": w1, "sel": sel.reshape(P, -1), "b2": b2,
             "wo": wo, "w2e": w2e, "wr": wr, "b1": b1, "iota": iota}
    wconst = np.concatenate([parts[n] for n in C_COLS], 1)

    arrays = {n: np.ascontiguousarray(a) for n, a in
              {"xin": xin, "wtok": wtok, "wqk": wqk, "wconst": wconst}.items()}
    nc = bacc.Bacc("TRN2", target_bir_lowering=False, num_devices=1)
    args = [nc.dram_tensor(n, a.shape, F32, kind="ExternalInput").ap() for n, a in arrays.items()]
    out = nc.dram_tensor("out", (TOK, D), F32, kind="ExternalOutput").ap()
    audio_tower(nc, *args, out)
    r = run_bass_kernel_spmd(nc, [arrays], core_ids=[0])
    return r.results[0]["out"].reshape(B, L, D)
```

```python
import numpy as np
from contextlib import ExitStack

import concourse.bass as bass
from concourse import mybir

F32 = mybir.dt.float32
F32R = mybir.dt.float32r
BF16 = mybir.dt.bfloat16
U32 = mybir.dt.uint32
ALU = mybir.AluOpType
ACT = mybir.ActivationFunctionType
AX = mybir.AxisListType

P = 128
B, DIMS, L, D = 16, 4, 256, 64
STEPS = 8
H, HG = 8, 4
E = 8
TOK = B * L
CH = 512
NCH = TOK // CH
BPC = CH // L
NT = TOK // P
UW = L + 2
EPS = 1e-5
MASKED = -1e30
ONE_ROW = 2 * DIMS
IN_ROWS = 32

W_COLS = {"wa": P, "w2": P, "wc": D, "w4": D}
C_COLS = {"ident": P, "w1": E * D, "sel": (E // 2) * P, "b2": P, "w2e": 4 * D, "wr": E,
          "b1": E // 2, "iota": E}
M_COLS = {"q": H * 2 * D, "k": H * D, "v": H * 2 * D, "o": H * D}


def places(widths):
    at, out = 0, {}
    for name, n in widths.items():
        out[name] = (at, at + n)
        at += n
    return out, at


W_AT, W_N = places(W_COLS)
C_AT, C_N = places(C_COLS)
M_AT, M_N = places(M_COLS)
A_G, A_V, A_S = 4, 2, 6
SUMS = 2 * H
PT_W = L + P


def audio_tower(nc, xin, wtok, wheads, wconst, out):
    ctx = ExitStack()
    with ctx:
        def sb(name, shape, dt=F32):
            return ctx.enter_context(nc.sbuf_tensor(name, shape, dt))

        def sem(name):
            return ctx.enter_context(nc.semaphore(name))

        xrows = sb("xrows", [P, TOK])
        tok_w = sb("tok_w", [P, W_N])
        const_w = sb("const_w", [P, C_N])
        drive = sb("drive", [P, TOK])
        state = sb("state", [P, B, UW])
        presum = sb("presum", [P, 4, CH])
        wg_high = sb("wg_high", [P, H, 2, D], F32R)
        wg_low = sb("wg_low", [P, H, 2, D], F32R)
        wv_high = sb("wv_high", [P, H * D], F32R)
        wv_low = sb("wv_low", [P, H * D], F32R)
        w1_high = sb("w1_high", [P, E * D], F32R)
        w1_low = sb("w1_low", [P, E * D], F32R)
        wr_high = sb("wr_high", [P, E], F32R)
        wr_low = sb("wr_low", [P, E], F32R)
        b2_high = sb("b2_high", [P, P], F32R)
        b2_low = sb("b2_low", [P, P], F32R)
        sel = sb("sel", [P, (E // 2) * P], F32R)
        ident_bf = sb("ident_bf", [P, P], BF16)
        causal_bf = sb("causal_bf", [P, 4, P], BF16)
        half = sb("half", [P, 2])
        mixedT = sb("mixedT", [D, L])
        h1 = sb("h1", [P, NT, D])
        base = h1
        stat_n = sb("stat_n", [P, 2, 6])
        mom_n = sb("mom_n", [P, 2, 2])
        var_n = sb("var_n", [P, 2])
        rstd_n = sb("rstd_n", [P, 2])
        xn = sb("xn", [P, 2, D])
        rowx = sb("rowx", [P, 2, 2 * D], F32R)
        xs = [sb(f"xs{q}", [P, L], F32R) for q in range(2)]
        g_h = sb("g_h", [P, H, L], F32R)
        g_l = sb("g_l", [P, H, L], F32R)
        vals = [sb(f"vals{q}", [P, 2, H * D]) for q in range(2)]
        negmax = sb("negmax", [P, 2, H])
        sums = sb("sums", [P, 2, H])
        rec = sb("rec", [P, 2, H])
        probs = sb("probs", [P, A_S, CH])
        pt = sb("pt", [P, H, PT_W])
        heads_w = pt[0:D, :, :].rearrange("p h w -> p (h w)")
        proj = sb("proj", [P, L])
        h2a = sb("h2a", [P, 2, D])
        h2 = sb("h2", [P, 2, D])
        stat_r = sb("stat_r", [P, 2, 6])
        mom_r = sb("mom_r", [P, 2, 2])
        var_r = sb("var_r", [P, 2])
        rstd_r = sb("rstd_r", [P, 2])
        yn = sb("yn", [P, 2, D])
        rowy = sb("rowy", [P, 2, 2 * D], F32R)
        ys = sb("ys", [P, L], F32R)
        ysall = sb("ysall", [P, TOK], F32R)
        srt = sb("srt", [P, 2, E])
        idx = sb("idx", [P, 2, E], U32)
        gap = sb("gap", [P, 2])
        egap = sb("egap", [P, 2])
        den = sb("den", [P, 2])
        wts = sb("wts", [P, 2, 2])
        hot = sb("hot", [P, 2, 2, E])
        hotw = sb("hotw", [P, 2, 2, E])
        comb = sb("comb", [P, 2, E])
        rowc = sb("rowc", [P, 2, 2 * E], F32R)
        combT = sb("combT", [P, TOK], F32R)
        hid = drive[:, 0:4 * CH].rearrange("p (t c) -> p t c", t=4)
        hidw = drive[:, 4 * CH:8 * CH].rearrange("p (t c) -> p t c", t=4)
        moe = presum[:, 0, :]
        outa = presum[:, 1, 0:CH // P * D].rearrange("p (t d) -> p t d", d=D)
        outb = presum[:, 2, 0:CH // P * D].rearrange("p (t d) -> p t d", d=D)

        def tw(name):
            a, z = W_AT[name]
            return tok_w[:, a:z]

        def cw(name):
            a, z = C_AT[name]
            return const_w[:, a:z]

        bank = [ctx.enter_context(nc.psum_tensor(f"bank{i}", [P, CH], F32)) for i in range(8)]
        key_bank = bank[0:4]
        prob_bank = bank[4:6]
        norm_bank, rout_bank = bank[6:8]

        x_in = [sem("x_in0"), sem("x_in1")]
        tok_in, heads_in, const_in = (sem(n) for n in ("tok_in", "heads_in", "const_in"))
        zeroed, zeroed_low, mask_zero, pool_consts, dve_consts, split_h, split_l = (
            sem(n) for n in ("zeroed", "zeroed_low", "mask_zero", "pool_consts", "dve_consts", "split_h", "split_l"))
        wg_mm, wg_h, wg_l, wv_h, wv_l = (sem(n) for n in ("wg_mm", "wg_h", "wg_l", "wv_h", "wv_l"))
        drive_mm, drive_copied = sem("drive_mm"), sem("drive_copied")
        step_mm, step_sum, state_ready, down_ready, edge_zero = (
            sem(n) for n in ("step_mm", "step_sum", "state_ready", "down_ready", "edge_zero"))
        mixed_mm, mixed_relu, mixedT_mm, h1_copied = (sem(n) for n in ("mixed_mm", "mixed_relu", "mixedT_mm", "h1_copied"))
        n_stats, n_moms, n_var, n_rstd, n_xn, n_high, n_low = (
            sem(n) for n in ("n_stats", "n_moms", "n_var", "n_rstd", "n_xn", "n_high", "n_low"))
        xs_mm, xs_copied = sem("xs_mm"), sem("xs_copied")
        g_mm, g_high, g_low, v_mm, v_copied, s_mm, s_max, s_sum, s_rec, s_scaled = (
            sem(n) for n in ("g_mm", "g_high", "g_low", "v_mm", "v_copied", "s_mm", "s_max", "s_sum", "s_rec",
                             "s_scaled"))
        pT_mm, pT_act, pT_dve, pv_mm = (sem(n) for n in ("pT_mm", "pT_act", "pT_dve", "pv_mm"))
        o_copied, oT_mm, r_h2a, r_h2, r_stats, r_moms, r_var, r_rstd, r_yn, r_high, r_low, r_base = (
            sem(n) for n in ("o_copied", "oT_mm", "r_h2a", "r_h2", "r_stats", "r_moms", "r_var", "r_rstd",
                             "r_yn", "r_high", "r_low", "r_base"))
        ys_mm, ys_copied, lg_mm, lg_sorted, lg_index, lg_gap, lg_exp, lg_den, lg_w0, lg_w1 = (
            sem(n) for n in ("ys_mm", "ys_copied", "lg_mm", "lg_sorted", "lg_index", "lg_gap", "lg_exp", "lg_den",
                             "lg_w0", "lg_w1"))
        c_hot, c_hotw, c_comb, c_high, c_low, c_mm, c_copied = (
            sem(n) for n in ("c_hot", "c_hotw", "c_comb", "c_high", "c_low", "c_mm", "c_copied"))
        up_mm, wt_mm, gelued, weighted, down_mm, moe_copied, moeT_mm, out_a, out_b, out_dma = (
            sem(n) for n in ("up_mm", "wt_mm", "gelued", "weighted", "down_mm", "moe_copied", "moeT_mm", "out_a",
                             "out_b", "out_dma"))

        def after(eng, signal, count, apart=False):
            if isinstance(count, int):
                if count > 0:
                    eng.wait_ge(signal, count)
                return
            if apart:
                count = eng.to_reg(count)
                eng.wait_ge(signal, 1)
            eng.wait_ge(signal, count)

        def exps_done(b, t):
            return SUMS * b + (4 * (t + 1) if t < 2 else 8 + 2 * (t - 1))

        def pT_places(copy, t):
            jb, nk, nh, n = blocks_of(t)
            cols = slice(0, P) if t < 2 else slice(P, PT_W)
            return copy(pt[:, n:n + nh, cols], prob_bank[t % 2][:, :].rearrange("p (h l) -> p h l", h=nh))

        def blocks_of(t):
            return (0, P, 4, 4 * t) if t < 2 else (1, L, 2, 2 * (t - 2))

        def pipeline(eng, step):
            def peeled(s):
                step(s, s % 2, [0 <= s - back < B for back in range(5)])
            for s in range(6):
                peeled(s)
            with eng.Fori(3, B // 2) as i:
                for q in range(2):
                    step(2 * i + q, q, [True] * 5)
            for s in range(B, B + 4):
                peeled(s)

        def chunks(eng, chunk):
            chunk(0)
            with eng.Fori(1, NCH) as k:
                chunk(k)
            chunk(NCH)

        seq2 = lambda c: slice(BPC * c, BPC * c + BPC)
        two = lambda ap: ap.rearrange("p (b l) -> p b l", b=BPC)

        block = ctx.enter_context(nc.Block())

        @block.sync
        def _(sp):
            sp.dma_start(tok_w[:, :], wtok).then_inc(tok_in, 16)
            for part in range(2):
                cols = slice(TOK // 2 * part, TOK // 2 * (part + 1))
                sp.dma_start(xrows[0:IN_ROWS, cols], xin[:, cols]).then_inc(x_in[part], 16)
            sp.dma_start(heads_w, wheads).then_inc(heads_in, 16)
            sp.dma_start(const_w[:, :], wconst).then_inc(const_in, 16)

            def chunk(k):
                if isinstance(k, int) and k == 0:
                    return
                sp.wait_ge(out_b, k)
                sp.dma_start(out[bass.ds((k - 1) * CH, CH), :].rearrange("(t p) d -> p t d", p=P),
                             outb).then_inc(out_dma, 16)
            chunks(sp, chunk)
            sp.wait_ge(out_dma, 16 * NCH)

        @block.gpsimd
        def _(pool):
            g = nc.gpsimd
            for part in range(2):
                g.memset(xrows[IN_ROWS:P // 2, TOK // 2 * part:TOK // 2 * (part + 1)], 0.0).then_inc(zeroed_low, 1)
            pool.wait_ge(zeroed_low, 2)
            g.memset(causal_bf[:, :, :], 0.0).then_inc(mask_zero, 1)
            g.memset(half[:, :], -0.5).then_inc(pool_consts, 1)
            pool.wait_ge(mask_zero, 1)
            g.affine_select(out=causal_bf[:, :, :], in_=causal_bf[:, :, :], compare_op=ALU.is_ge, fill=MASKED,
                            base=0, pattern=[[0, 4], [-1, P]], channel_multiplier=1).then_inc(pool_consts, 1)
            pool.wait_ge(const_in, 16)
            for high, low, w in ((wr_high, wr_low, "wr"), (w1_high, w1_low, "w1"),
                                 (b2_high, b2_low, "b2"), (sel, None, "sel")):
                g.tensor_copy(high[:, :], cw(w)).then_inc(split_h, 1)
            for n, (high, low, w) in enumerate(((wr_high, wr_low, "wr"), (w1_high, w1_low, "w1"),
                                                (b2_high, b2_low, "b2"))):
                pool.wait_ge(split_h, n + 1)
                g.tensor_tensor(low[:, :], cw(w), high[:, :].bitcast(F32), ALU.subtract).then_inc(split_l, 1)
            pool.wait_ge(pool_consts, 1)

            def rstd(b, moms, mom, var, s_var, rs, s_rstd):
                after(pool, moms, 2 * b + 2, apart=True)
                g.tensor_scalar(var[:, :], mom[:, :, 1], 1.0, EPS, ALU.mult, ALU.add).then_inc(s_var, 1)
                after(pool, s_var, b + 1)
                g.tensor_tensor(rs[:, :], var[:, :], half[:, :], ALU.pow).then_inc(s_rstd, 1)

            def scale(b, t):
                jb, nk, nh, n = blocks_of(t)
                after(pool, s_rec, 3 * b + t // 2 + 1, apart=True)
                v = probs[:, t, :].rearrange("p (h l) -> p h l", h=nh)
                g.tensor_tensor(v, v, rec[:, jb, n:n + nh].unsqueeze(2).broadcast_to([P, nh, nk]),
                                ALU.mult).then_inc(s_scaled, 1)

            def step(s, q, on):
                if on[4]:
                    b = s - 4
                    after(pool, c_hot, b + 1)
                    after(pool, lg_w1, b + 1)
                    g.tensor_tensor(hotw[:, :, :, :], hot[:, :, :, :],
                                    wts[:, :, :].unsqueeze(3).broadcast_to([P, 2, 2, E]),
                                    ALU.mult).then_inc(c_hotw, 1)
                    after(pool, c_hotw, b + 1)
                    after(pool, c_mm, b)
                    g.tensor_tensor(comb[:, :, :], hotw[:, :, 0, :], hotw[:, :, 1, :], ALU.add).then_inc(c_comb, 1)
                    after(pool, c_comb, b + 1, apart=True)
                    g.tensor_copy(rowc[:, :, 0:E], comb[:, :, :]).then_inc(c_high, 1)
                    after(pool, c_high, b + 1)
                    g.tensor_tensor(rowc[:, :, E:2 * E], comb[:, :, :], rowc[:, :, 0:E].bitcast(F32),
                                    ALU.subtract).then_inc(c_low, 1)
                if on[3]:
                    rstd(s - 3, r_moms, mom_r, var_r, r_var, rstd_r, r_rstd)
                if on[2]:
                    scale(s - 2, 4)
                    scale(s - 2, 5)
                if on[0]:
                    rstd(s, n_moms, mom_n, var_n, n_var, rstd_n, n_rstd)
                if on[3]:
                    b = s - 3
                    after(pool, r_yn, 2 * b + 2)
                    g.tensor_tensor(base[:, bass.ds(2 * b, 2), :], h2[:, :, :], yn[:, :, :],
                                    ALU.add).then_inc(r_base, 1)
                if on[1]:
                    for t in range(4):
                        scale(s - 1, t)

            pipeline(pool, step)

        @block.scalar
        def _(act):
            a = nc.scalar
            for c in range(NCH):
                act.wait_ge(drive_copied, c + 1)
                a.activation(state[:, seq2(c), 1:1 + L], two(bank[c][:, :]), ACT.Relu).then_inc(state_ready, 1)
            with act.Fori(0, STEPS - 2) as t:
                for c in range(NCH):
                    act.wait_ge(step_sum, NCH * t + c + 1)
                    a.activation(state[:, seq2(c), 1:1 + L], two(presum[:, c % 4, :]), ACT.Relu).then_inc(state_ready, 1)
            for c in range(NCH):
                act.wait_ge(step_sum, NCH * (STEPS - 2) + c + 1)
                a.activation(state[0:D, seq2(c), 1:1 + L], two(presum[0:D, c % 4, :]), ACT.Relu).then_inc(state_ready, 1)

            def g_high_part(b, t):
                after(act, g_mm, A_G * b + t + 1)
                a.activation(g_h[:, 2 * t:2 * t + 2, :], key_bank[t][:, :].rearrange("p (h l) -> p h l", h=2),
                             ACT.Copy).then_inc(g_high, 1)

            def pT_copy(b, t):
                after(act, pT_mm, A_S * b + t + 1)
                if t == 0:
                    after(act, pv_mm, b)
                pT_places(a.copy, t).then_inc(pT_act, 1)

            def v_copy(b, q, t):
                after(act, v_mm, A_V * b + t + 1)
                a.activation(vals[q][:, t, :], key_bank[t][:, :], ACT.Copy).then_inc(v_copied, 1)

            def exp_sums(b, t):
                after(act, s_max, A_S * b + t + 1)
                if t == 0:
                    after(act, s_rec, 3 * b)
                after(act, pT_mm, A_S * (b - 1) + t + 1)
                jb, nk, nh, n = blocks_of(t)
                for i in range(nh):
                    a.activation(probs[:, t, nk * i:nk * i + nk], key_bank[(t + 2) % 4][:, nk * i:nk * i + nk],
                                 ACT.Exp, bias=negmax[:, jb, n + i:n + i + 1],
                                 accum_out=sums[:, jb, n + i:n + i + 1]).then_inc(s_sum, 1)

            def step(s, q, on):
                r = 1 - q
                if on[4]:
                    b = s - 4
                    after(act, lg_gap, b + 1)
                    a.activation(egap[:, :], gap[:, :], ACT.Exp).then_inc(lg_exp, 1)
                if on[1]:
                    for t in range(2):
                        g_high_part(s - 1, t)
                if on[0]:
                    after(act, mixed_mm, s + 1)
                    a.activation(mixedT[:, :], norm_bank[0:D, 0:L], ACT.Relu).then_inc(mixed_relu, 1)
                if on[1]:
                    for t in range(2, A_G):
                        g_high_part(s - 1, t)
                if isinstance(s, int) and s == 0:
                    act.wait_ge(wg_mm, 1)
                    for i in range(2):
                        a.activation(wg_high[:, :, i, :], prob_bank[0][:, :].rearrange("p (h d) -> p h d", h=H),
                                     ACT.Copy).then_inc(wg_h, 1)
                    act.wait_ge(wg_mm, 2)
                    a.activation(wv_high[:, :], prob_bank[1][:, :], ACT.Copy).then_inc(wv_h, 1)
                for t in range(2):
                    if on[2]:
                        pT_copy(s - 2, t)
                    if on[1]:
                        v_copy(s - 1, r, t)
                if on[0]:
                    after(act, mixedT_mm, s + 1)
                    a.activation(h1[:, bass.ds(2 * s, 2), :],
                                 norm_bank[:, 0:2 * D].rearrange("p (t d) -> p t d", t=2), ACT.Copy).then_inc(h1_copied, 1)
                if on[2]:
                    pT_copy(s - 2, 2)
                if on[1]:
                    exp_sums(s - 1, 0)
                if on[4]:
                    b = s - 4
                    after(act, c_mm, b + 1)
                    a.activation(combT[0:2 * E, bass.ds(L * b, L)], rout_bank[0:2 * E, 0:L], ACT.Copy).then_inc(c_copied, 1)
                if on[1]:
                    exp_sums(s - 1, 1)
                    exp_sums(s - 1, 2)
                if on[3]:
                    b = s - 3
                    after(act, ys_mm, b + 1)
                    a.activation(ys[:, :], rout_bank[:, 0:L], ACT.Copy).then_inc(ys_copied, 1)
                    a.activation(ysall[:, bass.ds(L * b, L)], rout_bank[:, 0:L], ACT.Copy).then_inc(ys_copied, 1)
                if on[1]:
                    exp_sums(s - 1, 3)
                if on[0]:
                    after(act, xs_mm, s + 1)
                    a.activation(xs[q][:, :], norm_bank[:, 0:L], ACT.Copy).then_inc(xs_copied, 1)
                if on[1]:
                    exp_sums(s - 1, 4)
                    exp_sums(s - 1, 5)
                if on[2]:
                    b = s - 2
                    after(act, pv_mm, b + 1)
                    after(act, oT_mm, b)
                    a.activation(proj[:, :], prob_bank[0][:, 0:L], ACT.Copy).then_inc(o_copied, 1)

            pipeline(act, step)

            def chunk(k):
                if isinstance(k, int) and k == NCH:
                    act.wait_ge(down_mm, k)
                    act.wait_ge(moeT_mm, k - 1)
                    a.activation(moe, bank[4][:, :], ACT.Copy).then_inc(moe_copied, 1)
                    return
                for p in range(4):
                    after(act, up_mm, 4 * k + p + 1)
                    after(act, weighted, 4 * (k - 1) + p + 1)
                    a.activation(hid[:, p, :], bank[p % 2][:, :], ACT.Gelu, bias=cw("b1")[:, p:p + 1]).then_inc(gelued, 1)
                    if p == 1 and not (isinstance(k, int) and k == 0):
                        after(act, down_mm, k)
                        after(act, moeT_mm, k - 1)
                        a.activation(moe, bank[4][:, :], ACT.Copy).then_inc(moe_copied, 1)
            chunks(act, chunk)

        @block.vector
        def _(dve):
            v = nc.vector
            for part in range(2):
                v.memset(xrows[P // 2:P, TOK // 2 * part:TOK // 2 * (part + 1)], 0.0).then_inc(zeroed, 1)
            v.memset(state[:, :, 0:1], 0.0).then_inc(edge_zero, 1)
            for c in range(NCH):
                dve.wait_ge(drive_mm, c + 1)
                v.tensor_copy(drive[:, CH * c:CH * c + CH], bank[c][:, :]).then_inc(drive_copied, 1)
            v.memset(combT[:, :].bitcast(F32), 0.0).then_inc(dve_consts, 1)
            dve.wait_ge(const_in, 16)
            v.tensor_copy(ident_bf[:, :], cw("ident")).then_inc(dve_consts, 1)

            def step_presum(t, c):
                dve.wait_ge(step_mm, NCH * t + c + 1)
                dve.wait_ge(state_ready, NCH * t + c + 5)
                v.tensor_tensor(presum[:, c % 4, :], bank[c][:, :], drive[:, CH * c:CH * c + CH], ALU.add).then_inc(step_sum, 1)

            with dve.Fori(0, STEPS - 2) as t:
                for c in range(NCH):
                    step_presum(t, c)
            t = STEPS - 2
            for c in range(NCH):
                if c >= 4:
                    dve.wait_ge(down_ready, c - 3)
                step_presum(t, c)
                dve.wait_ge(step_sum, NCH * t + c + 1)
                v.tensor_scalar(state[D:P, seq2(c), L - 2::-1], two(presum[D:P, c % 4, :])[:, :, 0:L - 1], 0.0, None,
                                ALU.max).then_inc(down_ready, 1)
            v.memset(state[D:P, :, L - 1:L], 0.0).then_inc(down_ready, 1)

            def g_low_part(b, t):
                after(dve, g_high, A_G * b + t + 1)
                v.tensor_tensor(g_l[:, 2 * t:2 * t + 2, :], key_bank[t][:, :].rearrange("p (h l) -> p h l", h=2),
                                g_h[:, 2 * t:2 * t + 2, :].bitcast(F32), ALU.subtract).then_inc(g_low, 1)

            def pT_copy(b, t):
                after(dve, pT_mm, A_S * b + t + 1)
                if t == 3:
                    after(dve, pv_mm, b)
                pT_places(v.tensor_copy, t).then_inc(pT_dve, 1)

            def one_over_sums(b, t):
                jb, nk, nh, n = blocks_of(t)
                after(dve, s_sum, exps_done(b, t + 1))
                after(dve, s_scaled, A_S * (b - 1) + t + 2)
                v.reciprocal(rec[:, jb, n:n + 2 * nh], sums[:, jb, n:n + 2 * nh]).then_inc(s_rec, 1)

            def score_max(b, t):
                after(dve, s_mm, A_S * b + t + 1)
                jb, nk, nh, n = blocks_of(t)
                after(dve, s_sum, exps_done(b - 1, t))
                o, src = negmax[:, jb, n:n + nh], key_bank[(t + 2) % 4][:, :].rearrange("p (h l) -> p h l", h=nh)
                v.tensor_reduce(o, src, AX.X, ALU.max, negate=True).then_inc(s_max, 1)

            def moments(b, src, stat, s_stats, mom, s_moms):
                for t in range(2):
                    v.bn_stats(stat[:, t, :], src(t)).then_inc(s_stats, 1)
                for t in range(2):
                    after(dve, s_stats, 2 * b + t + 1, apart=True)
                    v.bn_aggr(mom[:, t, :], stat[:, t, :]).then_inc(s_moms, 1)

            def normed(b, src, mom, s_rstd, rs, o, s_o):
                after(dve, s_rstd, b + 1)
                for t in range(2):
                    v.tensor_scalar(o[:, t, :], src(t), mom[:, t, 0:1], rs[:, t:t + 1], ALU.subtract,
                                    ALU.mult).then_inc(s_o, 1)
                after(dve, s_o, 2 * b + 2)

            def step(s, q, on):
                r = 1 - q
                if on[4]:
                    b = s - 4
                    after(dve, lg_exp, b + 1)
                    v.tensor_scalar(den[:, :], egap[:, :], 1.0, None, ALU.add).then_inc(lg_den, 1)
                    after(dve, lg_den, b + 1)
                    v.reciprocal(wts[:, :, 0], den[:, :]).then_inc(lg_w0, 1)
                    after(dve, lg_w0, b + 1)
                    v.tensor_tensor(wts[:, :, 1], egap[:, :], wts[:, :, 0], ALU.mult).then_inc(lg_w1, 1)
                if on[1]:
                    g_low_part(s - 1, 0)
                    g_low_part(s - 1, 1)
                if on[3]:
                    b = s - 3
                    src = rout_bank[:, 0:2 * P].rearrange("p (t e) -> p t e", t=2)
                    after(dve, oT_mm, b + 1)
                    v.tensor_tensor(h2a[:, :, :], src[:, :, 0:D], h1[:, bass.ds(2 * b, 2), :], ALU.add).then_inc(r_h2a, 1)
                    after(dve, r_h2a, b + 1)
                    after(dve, r_base, b)
                    v.tensor_tensor(h2[:, :, :], src[:, :, D:P], h2a[:, :, :], ALU.add).then_inc(r_h2, 1)
                    after(dve, r_h2, b + 1)
                    moments(b, lambda t: h2[:, t, :], stat_r, r_stats, mom_r, r_moms)
                if on[1]:
                    g_low_part(s - 1, 2)
                    g_low_part(s - 1, 3)
                if on[3]:
                    b = s - 3
                    normed(b, lambda t: h2[:, t, :], mom_r, r_rstd, rstd_r, yn, r_yn)
                    v.tensor_copy(rowy[:, :, D:2 * D], yn[:, :, :]).then_inc(r_high, 1)
                    after(dve, r_high, b + 1)
                    v.tensor_tensor(rowy[:, :, 0:D], yn[:, :, :], rowy[:, :, D:2 * D].bitcast(F32),
                                    ALU.subtract).then_inc(r_low, 1)
                if isinstance(s, int) and s == 0:
                    dve.wait_ge(wg_h, 2)
                    for i in range(2):
                        v.tensor_tensor(wg_low[:, :, i, :], prob_bank[0][:, :].rearrange("p (h d) -> p h d", h=H),
                                        wg_high[:, :, i, :].bitcast(F32), ALU.subtract).then_inc(wg_l, 1)
                    dve.wait_ge(wv_h, 1)
                    v.tensor_tensor(wv_low[:, :], prob_bank[1][:, :], wv_high[:, :].bitcast(F32),
                                    ALU.subtract).then_inc(wv_l, 1)
                if on[1]:
                    score_max(s - 1, 0)
                if on[0]:
                    after(dve, h1_copied, s + 1)
                    moments(s, lambda t: h1[:, bass.ds(2 * s + t, 1), :].rearrange("p o d -> p (o d)"), stat_n,
                            n_stats, mom_n, n_moms)
                if on[1]:
                    score_max(s - 1, 1)
                    score_max(s - 1, 2)
                if on[2]:
                    pT_copy(s - 2, 3)
                    pT_copy(s - 2, 4)
                if on[1]:
                    score_max(s - 1, 3)
                if on[2]:
                    pT_copy(s - 2, 5)
                if on[0]:
                    normed(s, lambda t: h1[:, bass.ds(2 * s + t, 1), :].rearrange("p o d -> p (o d)"), mom_n, n_rstd,
                           rstd_n, xn, n_xn)
                    after(dve, xs_mm, s)
                    v.tensor_copy(rowx[:, :, D:2 * D], xn[:, :, :]).then_inc(n_high, 1)
                    after(dve, n_high, s + 1)
                    v.tensor_tensor(rowx[:, :, 0:D], xn[:, :, :], rowx[:, :, D:2 * D].bitcast(F32),
                                    ALU.subtract).then_inc(n_low, 1)
                if on[1]:
                    one_over_sums(s - 1, 0)
                    score_max(s - 1, 4)
                    one_over_sums(s - 1, 2)
                    score_max(s - 1, 5)
                if on[3]:
                    b = s - 3
                    after(dve, lg_mm, b + 1, apart=True)
                    for t in range(2):
                        v.max(srt[:, t, :], rout_bank[:, E * t:E * t + E]).then_inc(lg_sorted, 1)
                    for t in range(2):
                        after(dve, lg_sorted, 2 * b + t + 1, apart=True)
                        v.max_index(idx[:, t, :], srt[:, t, :], rout_bank[:, E * t:E * t + E]).then_inc(lg_index, 1)
                    after(dve, lg_exp, b)
                    v.tensor_tensor(gap[:, :], srt[:, :, 1], srt[:, :, 0], ALU.subtract).then_inc(lg_gap, 1)
                    after(dve, lg_index, 2 * b + 2)
                    after(dve, c_hotw, b)
                    v.tensor_tensor(hot[:, :, :, :], cw("iota").unsqueeze(1).unsqueeze(1).broadcast_to([P, 2, 2, E]),
                                    idx[:, :, 0:2].unsqueeze(3).broadcast_to([P, 2, 2, E]),
                                    ALU.is_equal).then_inc(c_hot, 1)
                if on[1]:
                    one_over_sums(s - 1, 4)

            pipeline(dve, step)

            def chunk(k):
                first = isinstance(k, int) and k == 0
                last = isinstance(k, int) and k == NCH

                def leave():
                    src = bank[5][:, :].rearrange("p (t e) -> p t e", t=CH // P)
                    after(dve, moeT_mm, k)
                    v.tensor_tensor(outa, src[:, :, 0:D], base[:, bass.ds((k - 1) * (CH // P), CH // P), :],
                                    ALU.add).then_inc(out_a, 1)
                    after(dve, out_a, k)
                    after(dve, out_dma, 16 * (k - 1))
                    v.tensor_tensor(outb, src[:, :, D:P], outa, ALU.add).then_inc(out_b, 1)
                if last:
                    leave()
                    return
                for p in range(4):
                    after(dve, gelued, 4 * k + p + 1)
                    after(dve, wt_mm, 4 * k + p + 1)
                    after(dve, down_mm, k)
                    v.tensor_tensor(hidw[:, p, :], bank[2 + p % 2][:, :], hid[:, p, :], ALU.mult).then_inc(weighted, 1)
                    if p == 3 and not first:
                        leave()
            chunks(dve, chunk)

        @block.tensor
        def _(pe):
            mm = nc.tensor.matmul
            ident = cw("ident")

            def tr(o, src):
                return nc.tensor.transpose(o, src.bitcast(F32), ident[0:src.shape[0], 0:src.shape[0]])

            pe.wait_ge(tok_in, 16)
            for c in range(NCH):
                if c % (NCH // 2) == 0:
                    part = c // (NCH // 2)
                    pe.wait_ge(x_in[part], 16)
                    pe.wait_ge(zeroed, part + 1)
                    pe.wait_ge(zeroed_low, part + 1)
                mm(bank[c][:, :], tw("wa"), xrows[:, CH * c:CH * c + CH], start=True, stop=True).then_inc(drive_mm, 1)
            pe.wait_ge(edge_zero, 1)
            with pe.Fori(0, STEPS - 1) as t:
                for c in range(NCH):
                    pe.wait_ge(state_ready, NCH * t + c + 1)
                    mm(bank[c][:, :], tw("w2"), state[:, seq2(c), 0:L], start=True, stop=True).then_inc(step_mm, 1)
            pe.wait_ge(state_ready, NCH * STEPS)
            pe.wait_ge(down_ready, NCH + 1)
            pe.wait_ge(pool_consts, 2)
            pe.wait_ge(dve_consts, 2)
            pe.wait_ge(split_h, 4)
            pe.wait_ge(split_l, 3)

            def heads_product():
                pe.wait_ge(heads_in, 16)
                for i, (left, right) in enumerate((("q", "k"), ("v", "o"))):
                    lw = heads_w[:, slice(*M_AT[left])].rearrange("p (h e) -> p h e", h=H)
                    rw = heads_w[:, slice(*M_AT[right])].rearrange("p (h e) -> p h e", h=H)
                    for n in range(H):
                        last = mm(prob_bank[i][:, n * D:n * D + D], lw[:, n, :], rw[:, n, :], start=True, stop=True)
                    last.then_inc(wg_mm, 1)

            def g_product(b, q, t):
                after(pe, s_sum, exps_done(b - 1, t + 2))
                for n in (2 * t, 2 * t + 1):
                    o = key_bank[t][:, L * (n % 2):L * (n % 2) + L]
                    mm(o, wg_high[:, n, :, :], xs[q][:, :], start=True, stop=False)
                    last = mm(o, wg_low[:, n, :, :], xs[q][:, :], start=False, stop=True)
                last.then_inc(g_mm, 1)

            def v_product(b, q, t):
                after(pe, g_low, A_G * b + t + 1)
                mm(key_bank[t][:, :], xs[q][:, P * t:P * t + P], wv_high[:, :], start=True, stop=False)
                mm(key_bank[t][:, :], xs[q][:, P * t:P * t + P], wv_low[:, :], start=False,
                   stop=True).then_inc(v_mm, 1)

            def score_product(b, q, t):
                if t < 2:
                    after(pe, g_low, A_G * b + 4)
                elif t < 4:
                    after(pe, v_copied, A_V * b + t - 1)
                else:
                    after(pe, s_sum, exps_done(b, t - 4))
                jb, nk, nh, n = blocks_of(t)
                o = key_bank[(t + 2) % 4][:, :].rearrange("p (h l) -> p h l", h=nh)
                mm(o, xs[q][:, P * jb:P * jb + P], g_h[:, n:n + nh, 0:nk], start=True, stop=False)
                mm(o, xs[q][:, P * jb:P * jb + P], g_l[:, n:n + nh, 0:nk], start=False, stop=False)
                mm(o[:, :, nk - P:nk], ident_bf[:, :], causal_bf[:, 0:nh, :], start=False, stop=True).then_inc(s_mm, 1)

            def prob_turn(b, t):
                if t == 0:
                    after(pe, o_copied, b)
                after(pe, s_scaled, A_S * b + t + 1)
                if t < 2:
                    after(pe, pT_dve, 3 * (b - 1) + t + 2)
                elif t < 5:
                    after(pe, pT_act, 3 * b + t - 1)
                else:
                    after(pe, pT_dve, 3 * b + 1)
                for i in range(CH // P):
                    last = tr(prob_bank[t % 2][:, P * i:P * i + P], probs[:, t, P * i:P * i + P])
                last.then_inc(pT_mm, 1)

            def value_product(b, q, grp):
                if grp == 0:
                    after(pe, pT_act, 3 * b + 3)
                    after(pe, pT_dve, 3 * b + 3)
                for n in range(HG * grp, HG * grp + HG, 2):
                    for kb in range(2):
                        for i in range(2):
                            last = mm(prob_bank[0][D * i:D * i + D, P * kb:L],
                                      vals[q][:, kb, D * (n + i):D * (n + i) + D],
                                      pt[:, n + i, L * kb:L * kb + L - P * kb], start=(n == 0 and kb == 0),
                                      stop=(n == H - 2 and kb == 1))
                if grp == 1:
                    last.then_inc(pv_mm, 1)

            def step(s, q, on):
                r = 1 - q
                if on[1]:
                    after(pe, xs_copied, s)
                    if isinstance(s, int) and s == 1:
                        pe.wait_ge(wg_l, 2)
                        pe.wait_ge(wv_l, 1)
                    g_product(s - 1, r, 0)
                    g_product(s - 1, r, 1)
                if on[0]:
                    after(pe, xs_copied, s)
                    o = norm_bank[0:D, 0:L]
                    mm(o, tw("wc"), xrows[:, bass.ds(L * s, L)], start=True, stop=False)
                    mm(o, tw("w4"), state[:, bass.ds(s, 1), 0:L].rearrange("p o l -> p (o l)"), start=False,
                       stop=True).then_inc(mixed_mm, 1)
                if on[3]:
                    after(pe, o_copied, s - 2)
                    after(pe, lg_index, 2 * (s - 3))
                    for t in range(2):
                        last = tr(rout_bank[:, P * t:P * t + P], proj[:, P * t:P * t + P])
                    last.then_inc(oT_mm, 1)
                if on[1]:
                    g_product(s - 1, r, 2)
                    g_product(s - 1, r, 3)
                if isinstance(s, int) and s == 0:
                    heads_product()
                for t in range(2):
                    if on[2]:
                        prob_turn(s - 2, t)
                    if on[1]:
                        v_product(s - 1, r, t)
                if on[0]:
                    after(pe, mixed_relu, s + 1, apart=True)
                    for t in range(2):
                        last = tr(norm_bank[:, D * t:D * t + D], mixedT[:, P * t:P * t + P])
                    last.then_inc(mixedT_mm, 1)
                if on[2]:
                    prob_turn(s - 2, 2)
                for t in range(2):
                    if on[1]:
                        score_product(s - 1, r, t)
                if on[2]:
                    prob_turn(s - 2, 3)
                if on[4]:
                    b = s - 4
                    after(pe, c_low, b + 1)
                    after(pe, r_h2 if on[3] else lg_index, b + 2 if on[3] else 2 * B)
                    for t in range(2):
                        last = tr(rout_bank[0:2 * E, P * t:P * t + P], rowc[:, t, :])
                    last.then_inc(c_mm, 1)
                if on[1]:
                    score_product(s - 1, r, 2)
                if on[2]:
                    prob_turn(s - 2, 4)
                if on[1]:
                    score_product(s - 1, r, 3)
                if on[3]:
                    b = s - 3
                    after(pe, r_low, b + 1)
                    after(pe, c_copied, b)
                    for t in range(2):
                        last = tr(rout_bank[:, P * t:P * t + P], rowy[:, t, :])
                    last.then_inc(ys_mm, 1)
                if on[2]:
                    prob_turn(s - 2, 5)
                if on[1]:
                    score_product(s - 1, r, 4)
                if on[2]:
                    value_product(s - 2, q, 0)
                if on[0]:
                    after(pe, n_low, s + 1)
                    for t in range(2):
                        last = tr(norm_bank[:, P * t:P * t + P], rowx[:, t, :])
                    last.then_inc(xs_mm, 1)
                if on[1]:
                    score_product(s - 1, r, 5)
                if on[3]:
                    b = s - 3
                    after(pe, ys_copied, 2 * b + 2)
                    for t in range(2):
                        o = rout_bank[:, E * t:E * t + E]
                        mm(o, ys[:, P * t:P * t + P], wr_high[:, :], start=True, stop=False)
                        last = mm(o, ys[:, P * t:P * t + P], wr_low[:, :], start=False, stop=True)
                    last.then_inc(lg_mm, 1)
                if on[2]:
                    value_product(s - 2, q, 1)

            pipeline(pe, step)

            pe.wait_ge(c_copied, B)
            pe.wait_ge(s_sum, SUMS * B)
            pe.wait_ge(pT_dve, 3 * B)

            def up(k, p):
                after(pe, gelued, 4 * k + p - 1)
                cols = bass.ds(CH * k, CH)
                mm(bank[p % 2][:, :], w1_high[:, P * p:P * p + P], ysall[:, cols], start=True, stop=False)
                mm(bank[p % 2][:, :], w1_low[:, P * p:P * p + P], ysall[:, cols], start=False,
                   stop=True).then_inc(up_mm, 1)
                after(pe, weighted, 4 * k + p - 1)
                mm(bank[2 + p % 2][:, :], sel[:, P * p:P * p + P], combT[:, cols], start=True, stop=True).then_inc(wt_mm, 1)

            def down(k, p):
                if p == 0:
                    after(pe, moe_copied, k)
                    cols = bass.ds(CH * k, CH)
                    mm(bank[4][:, :], b2_high[:, :], combT[:, cols], start=True, stop=False)
                    mm(bank[4][:, :], b2_low[:, :], combT[:, cols], start=False, stop=False)
                half_rows = slice(D * (p // 2), D * (p // 2) + D)
                after(pe, weighted, 4 * k + p + 1)
                last = mm(bank[4][half_rows, :], cw("w2e")[:, D * p:D * p + D], hidw[:, p, :], start=False,
                          stop=(p % 2 == 1))
                if p == 3:
                    last.then_inc(down_mm, 1)

            def turn(k):
                after(pe, moe_copied, k)
                after(pe, out_b, k - 1)
                for t in range(CH // P):
                    last = tr(bank[5][:, P * t:P * t + P], moe[:, P * t:P * t + P])
                last.then_inc(moeT_mm, 1)

            def chunk(k):
                first = isinstance(k, int) and k == 0
                if isinstance(k, int) and k == NCH:
                    down(k - 1, 2)
                    down(k - 1, 3)
                    turn(k)
                    return
                for p in range(4):
                    up(k, p)
                    if p < 2 and not first:
                        down(k - 1, p + 2)
                    if p == 3 and not first:
                        turn(k)
                    if p >= 2:
                        down(k, p - 2)
            chunks(pe, chunk)


def kernel(**inputs):
    import concourse.bacc as bacc
    from concourse.bass_utils import run_bass_kernel_spmd

    f = {k: np.asarray(v) for k, v in inputs.items()}
    z = lambda *shape: np.zeros(shape, np.float32)
    x = f["x"].transpose(1, 0, 2)
    xin = z(IN_ROWS, TOK)
    xin[0:2 * DIMS] = np.concatenate([x, x[:, :, ::-1]], 0).reshape(2 * DIMS, TOK)
    xin[ONE_ROW:ONE_ROW + 3] = 1.0

    wa = z(P, P)
    wa[0:DIMS, 0:D] = wa[DIMS:2 * DIMS, D:P] = f["L0_tok_W1"].T
    for i, name in enumerate(("L0_tok_b1", "L0_tok_b2")):
        wa[ONE_ROW + i] = np.concatenate([f[name], f[name]])
    w2 = z(P, P)
    w2[0:D, 0:D] = w2[D:P, D:P] = f["L0_tok_W2"].T
    wc = z(P, D)
    wc[0:DIMS] = f["L0_tok_W3"].T
    for i, name in enumerate(("L0_tok_b3", "L0_tok_b4", "L0_tok_b4")):
        wc[ONE_ROW + i] = f[name]
    w4 = np.concatenate([f["L0_tok_W4"].T] * 2, 0)
    wtok = np.concatenate([wa, w2, wc, w4], 1)

    q, k, v = (f[f"L0_attn_{n}_matrices"].transpose(2, 0, 1) for n in ("query", "key", "value_in"))
    o = f["L0_attn_value_out_matrices"].transpose(1, 0, 2)
    twice = lambda a: np.concatenate([a, a], 2)
    wheads = np.concatenate([a.reshape(D, -1) for a in (twice(q), k, twice(v), o)], 1)

    double = lambda a: np.concatenate([a, a], 0)
    w1 = double(f["L0_ffn_w1"].transpose(1, 0, 2).reshape(D, E * D))
    wr = double(f["L0_ffn_router_w"].T)
    sel = z(P, E // 2, 2, D)
    for e in range(E):
        sel[e, e // 2, e % 2] = sel[E + e, e // 2, e % 2] = 1.0
    b2 = z(P, P)
    b2[0:E, 0:D] = b2[E:2 * E, 0:D] = f["L0_ffn_b2"]
    w2e = f["L0_ffn_w2"].reshape(E // 2, P, D).transpose(1, 0, 2).reshape(P, 4 * D)
    b1 = f["L0_ffn_b1"].reshape(E // 2, P).T
    iota = np.tile(np.arange(E, dtype=np.float32), (P, 1))
    parts = {"ident": np.eye(P, dtype=np.float32), "w1": w1, "sel": sel.reshape(P, -1), "b2": b2, "w2e": w2e,
             "wr": wr, "b1": b1, "iota": iota}
    wconst = np.concatenate([parts[n] for n in C_COLS], 1)

    arrays = {n: np.ascontiguousarray(a) for n, a in
              {"xin": xin, "wtok": wtok, "wheads": wheads, "wconst": wconst}.items()}
    nc = bacc.Bacc("TRN2", target_bir_lowering=False, num_devices=1)
    args = [nc.dram_tensor(n, a.shape, F32, kind="ExternalInput").ap() for n, a in arrays.items()]
    out = nc.dram_tensor("out", (TOK, D), F32, kind="ExternalOutput").ap()
    audio_tower(nc, *args, out)
    r = run_bass_kernel_spmd(nc, [arrays], core_ids=[0])
    return r.results[0]["out"].reshape(B, L, D)
```

```python
import math
from contextlib import ExitStack

import numpy as np

import concourse.bass as bass
from concourse import mybir

F32 = mybir.dt.float32
F32R = mybir.dt.float32r
BF16 = mybir.dt.bfloat16
U32 = mybir.dt.uint32
ALU = mybir.AluOpType
ACT = mybir.ActivationFunctionType
AX = mybir.AxisListType

P = 128
B, DIMS, L, D = 16, 4, 256, 64
STEPS = 8
H, HG = 8, 4
E = 8
TOK = B * L
CH = 512
NCH = TOK // CH
BPC = CH // L
NT = TOK // P
UW = L + 2
EPS = 1e-5
MASKED = -1e30
ONE_ROW = 2 * DIMS
IN_ROWS = 32

W_COLS = {"wa": P, "w2": P, "wc": D, "w4": D}
C_COLS = {"ident": P, "w1": E * D, "sel": (E // 2) * P, "b2": P, "b2l": P, "w2e": 4 * D, "wr": E,
          "b1": E // 2, "iota": E}
M_COLS = {"q": H * 2 * D, "k": H * D, "v": H * 2 * D, "o": H * D}


def places(widths):
    at, out = 0, {}
    for name, n in widths.items():
        out[name] = (at, at + n)
        at += n
    return out, at


W_AT, W_N = places(W_COLS)
C_AT, C_N = places(C_COLS)
M_AT, M_N = places(M_COLS)
A_G, A_V, A_S = 4, 2, 6
X_PARTS = (0, CH, TOK)
EARLY = 4
M_FIRST = 6
SUMS = 2 * H
PT_W = L + P


def audio_tower(nc, xin, wtok, wheads, wconst, out):
    ctx = ExitStack()
    with ctx:
        def sb(name, shape, dt=F32):
            return ctx.enter_context(nc.sbuf_tensor(name, shape, dt))

        def sem(name):
            return ctx.enter_context(nc.semaphore(name))

        xrows = sb("xrows", [P, TOK])
        tok_w = sb("tok_w", [P, W_N])
        const_w = sb("const_w", [P, C_N])
        drive = sb("drive", [P, TOK])
        state = sb("state", [P, B, UW])
        presum = sb("presum", [P, 4, CH])
        wg_high = sb("wg_high", [P, H, 2, D], F32R)
        wg_low = sb("wg_low", [P, H, 2, D], F32R)
        wv_high = sb("wv_high", [P, H * D], F32R)
        wv_low = sb("wv_low", [P, H * D], F32R)
        w1_high = sb("w1_high", [P, E * D], F32R)
        w1_low = sb("w1_low", [P, E * D], F32R)
        wr_high = sb("wr_high", [P, E], F32R)
        wr_low = sb("wr_low", [P, E], F32R)
        b2_high = sb("b2_high", [P, P], F32R)
        b2_high_l = sb("b2_high_l", [P, P], F32R)
        b2_low = sb("b2_low", [P, P], F32R)
        b2_parts = sb("b2_parts", [P, P], F32R)
        sel = sb("sel", [P, (E // 2) * P], F32R)
        ident_bf = sb("ident_bf", [P, P], BF16)
        causal_bf = sb("causal_bf", [P, 4, P], BF16)
        half = sb("half", [P, 2])
        euler = sb("euler", [P, 2])
        h1 = sb("h1", [P, NT, D])
        base = h1
        stat_n = sb("stat_n", [P, 2, 6])
        mom_n = sb("mom_n", [P, 2, 2])
        var_n = sb("var_n", [P, 2])
        rstd_n = sb("rstd_n", [P, 2])
        xn = sb("xn", [P, 2, D])
        rowx = sb("rowx", [P, 2, 2 * D], F32R)
        xs = [sb(f"xs{q}", [P, L], F32R) for q in range(2)]
        g_h = sb("g_h", [P, H, L], F32R)
        g_l = sb("g_l", [P, H, L], F32R)
        vals = [sb(f"vals{q}", [P, 2, H * D]) for q in range(2)]
        negmax = sb("negmax", [P, 2, H])
        sums = sb("sums", [P, 2, H])
        rec = sb("rec", [P, 2, H])
        probs = sb("probs", [P, A_S, CH])
        pt = sb("pt", [P, H, PT_W])
        heads_w = pt[0:D, :, :].rearrange("p h w -> p (h w)")
        proj = sb("proj", [P, L])
        h2a = sb("h2a", [P, 2, D])
        h2 = sb("h2", [P, 2, D])
        stat_r = sb("stat_r", [P, 2, 6])
        mom_r = sb("mom_r", [P, 2, 2])
        var_r = sb("var_r", [P, 2])
        rstd_r = sb("rstd_r", [P, 2])
        yn = sb("yn", [P, 2, D])
        rowy = sb("rowy", [P, 2, 2 * D], F32R)
        ys = sb("ys", [P, L], F32R)
        ysall = sb("ysall", [P, TOK], F32R)
        srt = sb("srt", [P, 2, E])
        idx = sb("idx", [P, 2, E], U32)
        gap = sb("gap", [P, 2])
        egap = sb("egap", [P, 2])
        den = sb("den", [P, 2])
        wts = sb("wts", [P, 2, 2])
        hot = sb("hot", [P, 2, 2, E])
        hotw = sb("hotw", [P, 2, 2, E])
        comb = sb("comb", [P, 2, E])
        rowc = sb("rowc", [P, 2, 2, 2 * E], F32R)
        combT = sb("combT", [P, TOK], F32R)
        mixedT = drive[:, 0:B // 2 * L].rearrange("p (c l) -> p c l", c=B // 2)
        hid = drive[:, 0:4 * CH].rearrange("p (t c) -> p t c", t=4)
        hidw = drive[:, 4 * CH:8 * CH].rearrange("p (t c) -> p t c", t=4)
        moe = presum[:, 0, :]
        outa = presum[:, 1, 0:CH // P * D].rearrange("p (t d) -> p t d", d=D)
        outb = presum[:, 2, 0:CH // P * D].rearrange("p (t d) -> p t d", d=D)

        def tw(name):
            a, z = W_AT[name]
            return tok_w[:, a:z]

        def cw(name):
            a, z = C_AT[name]
            return const_w[:, a:z]

        bank = [ctx.enter_context(nc.psum_tensor(f"bank{i}", [P, CH], F32)) for i in range(8)]
        up_bank, wt_bank, moe_bank, turn_bank = bank[0:2], bank[2:4], bank[6], bank[5]
        key_bank = bank[0:4]
        prob_bank = bank[4:6]
        norm_bank, rout_bank = bank[6:8]

        x_in = [sem("x_in0"), sem("x_in1")]
        tok_in, heads_in, const_in = (sem(n) for n in ("tok_in", "heads_in", "const_in"))
        zeroed, zeroed_low, mask_zero, pool_consts, dve_consts, split_h, split_l = (
            sem(n) for n in ("zeroed", "zeroed_low", "mask_zero", "pool_consts", "dve_consts", "split_h", "split_l"))
        wg_mm, wg_h, wg_l, wv_h, wv_l = (sem(n) for n in ("wg_mm", "wg_h", "wg_l", "wv_h", "wv_l"))
        drive_mm, drive_copied = sem("drive_mm"), sem("drive_copied")
        step_mm, step_sum, state_ready, down_even, down_odd, down_edge, edge_zero = (
            sem(n) for n in ("step_mm", "step_sum", "state_ready", "down_even", "down_odd", "down_edge", "edge_zero"))
        mixed_mm, mixed_relu, mixedT_mm, h1_copied = (sem(n) for n in ("mixed_mm", "mixed_relu", "mixedT_mm", "h1_copied"))
        n_stats, n_moms, n_var, n_rstd, n_xn, n_high, n_low = (
            sem(n) for n in ("n_stats", "n_moms", "n_var", "n_rstd", "n_xn", "n_high", "n_low"))
        xs_mm, xs_copied = sem("xs_mm"), sem("xs_copied")
        g_mm, g_high, g_low, v_mm, v_copied, s_mm, s_max, s_sum, s_rec, s_scaled = (
            sem(n) for n in ("g_mm", "g_high", "g_low", "v_mm", "v_copied", "s_mm", "s_max", "s_sum", "s_rec",
                             "s_scaled"))
        pT_mm, pT_act, pT_dve, pv_mm = (sem(n) for n in ("pT_mm", "pT_act", "pT_dve", "pv_mm"))
        o_copied, oT_mm, r_h2a, r_h2, r_stats, r_moms, r_var, r_rstd, r_yn, r_high, r_low, r_base = (
            sem(n) for n in ("o_copied", "oT_mm", "r_h2a", "r_h2", "r_stats", "r_moms", "r_var", "r_rstd",
                             "r_yn", "r_high", "r_low", "r_base"))
        ys_mm, ys_copied, lg_mm, lg_sorted, lg_index, lg_gap, lg_exp, lg_den, lg_w0, lg_w1 = (
            sem(n) for n in ("ys_mm", "ys_copied", "lg_mm", "lg_sorted", "lg_index", "lg_gap", "lg_exp", "lg_den",
                             "lg_w0", "lg_w1"))
        c_hot, c_hotw, c_comb, c_high, c_low, c_mm, c_copied = (
            sem(n) for n in ("c_hot", "c_hotw", "c_comb", "c_high", "c_low", "c_mm", "c_copied"))
        up_mm, wt_mm, gelued, weighted, down_a, down_mm, moe_copied, moeT_mm, out_a, out_b, out_dma = (
            sem(n) for n in ("up_mm", "wt_mm", "gelued", "weighted", "down_a", "down_mm", "moe_copied", "moeT_mm", "out_a",
                             "out_b", "out_dma"))

        def after(eng, signal, count, apart=False):
            if isinstance(count, int):
                if count > 0:
                    eng.wait_ge(signal, count)
                return
            if apart:
                count = eng.to_reg(count)
                eng.wait_ge(signal, 1)
            eng.wait_ge(signal, count)

        def exps_done(b, t):
            return SUMS * b + (4 * (t + 1) if t < 2 else 8 + 2 * (t - 1))

        def pT_places(copy, t):
            jb, nk, nh, n = blocks_of(t)
            cols = slice(0, P) if t < 2 else slice(P, PT_W)
            return copy(pt[:, n:n + nh, cols], prob_bank[t % 2][:, :].rearrange("p (h l) -> p h l", h=nh))

        def mixed_bank(c):
            return key_bank[c % 4] if c < M_FIRST else prob_bank[c % 2]

        def blocks_of(t):
            return (0, P, 4, 4 * t) if t < 2 else (1, L, 2, 2 * (t - 2))

        def pipeline(eng, step):
            def peeled(s):
                step(s, s % 2, [0 <= s - back < B for back in range(5)])
            for s in range(6):
                peeled(s)
            with eng.Fori(3, B // 2) as i:
                for q in range(2):
                    step(2 * i + q, q, [True] * 5)
            for s in range(B, B + 4):
                peeled(s)

        def chunks(eng, chunk):
            with eng.Fori(EARLY, NCH) as k:
                chunk(k)
            chunk(NCH)

        seq2 = lambda c: slice(BPC * c, BPC * c + BPC)
        two = lambda ap: ap.rearrange("p (b l) -> p b l", b=BPC)

        block = ctx.enter_context(nc.Block())

        @block.sync
        def _(sp):
            for part in range(2):
                cols = slice(*X_PARTS[part:part + 2])
                sp.dma_start(xrows[0:IN_ROWS, cols], xin[:, cols]).then_inc(x_in[part], 16)
            sp.dma_start(heads_w, wheads).then_inc(heads_in, 16)
            sp.dma_start(const_w[:, :], wconst).then_inc(const_in, 16)

            def chunk(k):
                sp.wait_ge(out_b, k)
                sp.dma_start(out[bass.ds((k - 1) * CH, CH), :].rearrange("(t p) d -> p t d", p=P),
                             outb).then_inc(out_dma, 16)
            for k in range(1, EARLY):
                chunk(k)
            chunks(sp, chunk)
            sp.wait_ge(out_dma, 16 * NCH)

        @block.gpsimd
        def _(pool):
            g = nc.gpsimd
            for part in range(2):
                g.memset(xrows[IN_ROWS:P // 2, slice(*X_PARTS[part:part + 2])], 0.0).then_inc(zeroed_low, 1)
            pool.wait_ge(zeroed_low, 2)
            g.memset(causal_bf[:, :, :], 0.0).then_inc(mask_zero, 1)
            g.memset(half[:, :], -0.5).then_inc(pool_consts, 1)
            g.memset(euler[:, :], math.e).then_inc(pool_consts, 1)
            pool.wait_ge(mask_zero, 1)
            g.affine_select(out=causal_bf[:, :, :], in_=causal_bf[:, :, :], compare_op=ALU.is_ge, fill=MASKED,
                            base=0, pattern=[[0, 4], [-1, P]], channel_multiplier=1).then_inc(pool_consts, 1)
            pool.wait_ge(const_in, 16)
            for high, low, w in ((wr_high, wr_low, "wr"), (w1_high, w1_low, "w1"),
                                 (b2_high_l, b2_low, "b2l"), (b2_high, None, "b2"), (sel, None, "sel")):
                g.tensor_copy(high[:, :], cw(w)).then_inc(split_h, 1)
            for n, (high, low, w) in enumerate(((wr_high, wr_low, "wr"), (w1_high, w1_low, "w1"),
                                                (b2_high_l, b2_low, "b2l"))):
                pool.wait_ge(split_h, n + 1)
                g.tensor_tensor(low[:, :], cw(w), high[:, :].bitcast(F32), ALU.subtract).then_inc(split_l, 1)
            pool.wait_ge(split_l, 3)
            pool.wait_ge(split_h, 4)
            g.tensor_tensor(b2_parts[:, :], b2_high[:, :].bitcast(F32), b2_low[:, :].bitcast(F32),
                            ALU.add).then_inc(split_l, 1)
            pool.wait_ge(pool_consts, 2)
            pool.wait_ge(step_mm, NCH * (STEPS - 1))
            pool.wait_ge(split_l, 4)
            g.memset(state[D:P, :, L - 1:L], 0.0).then_inc(down_edge, 1)
            pool.wait_ge(down_edge, 1)

            def rstd(b, moms, mom, var, s_var, rs, s_rstd):
                after(pool, moms, 2 * b + 2, apart=True)
                g.tensor_scalar(var[:, :], mom[:, :, 1], 1.0, EPS, ALU.mult, ALU.add).then_inc(s_var, 1)
                after(pool, s_var, b + 1)
                g.tensor_tensor(rs[:, :], var[:, :], half[:, :], ALU.pow).then_inc(s_rstd, 1)

            def scale(b, t):
                jb, nk, nh, n = blocks_of(t)
                after(pool, s_rec, 3 * b + t // 2 + 1, apart=True)
                v = probs[:, t, :].rearrange("p (h l) -> p h l", h=nh)
                g.tensor_tensor(v, v, rec[:, jb, n:n + nh].unsqueeze(2).broadcast_to([P, nh, nk]),
                                ALU.mult).then_inc(s_scaled, 1)

            def rstd_first(b):
                rstd(b, n_moms, mom_n, var_n, n_var, rstd_n, n_rstd)

            def first_parts(b):
                after(pool, n_xn, 2 * b + 2, apart=True)
                after(pool, xs_mm, b, apart=True)
                g.tensor_copy(rowx[:, :, D:2 * D], xn[:, :, :]).then_inc(n_high, 1)
                after(pool, n_high, b + 1)
                g.tensor_tensor(rowx[:, :, 0:D], xn[:, :, :], rowx[:, :, D:2 * D].bitcast(F32),
                                ALU.subtract).then_inc(n_low, 1)

            def rstd_second(b):
                rstd(b, r_moms, mom_r, var_r, r_var, rstd_r, r_rstd)

            def gap_exp(b):
                after(pool, lg_gap, b + 1)
                g.tensor_tensor(egap[:, :], euler[:, :], gap[:, :], ALU.pow).then_inc(lg_exp, 1)

            def routing_rows(b):
                after(pool, c_hot, b + 1)
                after(pool, lg_w1, b + 1)
                g.tensor_tensor(hotw[:, :, :, :], hot[:, :, :, :],
                                wts[:, :, :].unsqueeze(3).broadcast_to([P, 2, 2, E]),
                                ALU.mult).then_inc(c_hotw, 1)
                after(pool, c_hotw, b + 1)
                after(pool, c_mm, b)
                g.tensor_tensor(comb[:, :, :], hotw[:, :, 0, :], hotw[:, :, 1, :], ALU.add).then_inc(c_comb, 1)
                after(pool, c_comb, b + 1, apart=True)
                both = comb[:, :, :].unsqueeze(2).broadcast_to([P, 2, 2, E])
                g.tensor_copy(rowc[:, :, :, 0:E], both).then_inc(c_high, 1)
                after(pool, c_high, b + 1)
                g.tensor_tensor(rowc[:, :, :, E:2 * E], both, rowc[:, :, :, 0:E].bitcast(F32),
                                ALU.subtract).then_inc(c_low, 1)

            def base_rows(b):
                after(pool, r_yn, 2 * b + 2)
                g.tensor_tensor(base[:, bass.ds(2 * b, 2), :], h2[:, :, :], yn[:, :, :],
                                ALU.add).then_inc(r_base, 1)

            def step(s, q, on):
                def run(stage, piece, *args):
                    if on[stage]:
                        piece(s - stage, *args)
                run(2, scale, 4)
                run(0, rstd_first)
                run(4, gap_exp)
                run(3, rstd_second)
                run(2, scale, 5)
                run(0, first_parts)
                run(4, routing_rows)
                for t in range(3):
                    run(1, scale, t)
                run(3, base_rows)
                run(1, scale, 3)

            pipeline(pool, step)

        @block.scalar
        def _(act):
            a = nc.scalar
            act.dma_start(tok_w[:, :], wtok).then_inc(tok_in, 16)
            for c in range(NCH):
                act.wait_ge(drive_copied, c + 1)
                a.activation(state[:, seq2(c), 1:1 + L], two(bank[c][:, :]), ACT.Relu).then_inc(state_ready, 1)
            with act.Fori(0, STEPS - 2) as t:
                for c in range(NCH):
                    act.wait_ge(step_sum, NCH * t + c + 1)
                    a.activation(state[:, seq2(c), 1:1 + L], two(presum[:, c % 4, :]), ACT.Relu).then_inc(state_ready, 1)
            for c in range(NCH):
                act.wait_ge(step_sum, NCH * (STEPS - 2) + c + 1)
                a.activation(state[0:D, seq2(c), 1:1 + L], two(presum[0:D, c % 4, :]), ACT.Relu).then_inc(state_ready, 1)
                if c % 2:
                    a.activation(state[D:P, seq2(c), L - 2::-1], two(presum[D:P, c % 4, :])[:, :, 0:L - 1],
                                 ACT.Relu).then_inc(down_odd, 1)

            def mixed_part(c):
                act.wait_ge(mixed_mm, c + 1)
                act.wait_ge(step_sum, NCH * (STEPS - 1))
                a.activation(mixedT[:, c, :], mixed_bank(c)[:, 0:L], ACT.Relu).then_inc(mixed_relu, 1)

            def h1_part(c):
                act.wait_ge(mixedT_mm, c + 1)
                a.activation(h1[:, 4 * c:4 * c + 4, :].rearrange("p (i t) d -> p i t d", i=2),
                             rout_bank[:, 0:L].rearrange("p (t i d) -> p i t d", t=2, i=2),
                             ACT.Copy).then_inc(h1_copied, 1)

            act.wait_ge(wg_mm, 1)
            for i in range(2):
                a.activation(wg_high[:, :, i, :], prob_bank[0][:, :].rearrange("p (h d) -> p h d", h=H),
                             ACT.Copy).then_inc(wg_h, 1)
            mixed_part(0)
            mixed_part(1)
            h1_part(0)
            act.wait_ge(wg_mm, 2)
            a.activation(wv_high[:, :], prob_bank[1][:, :], ACT.Copy).then_inc(wv_h, 1)
            h1_part(1)
            for c in range(2, M_FIRST):
                mixed_part(c)
                if c < M_FIRST - 1:
                    h1_part(c)

            def g_high_part(b, t):
                after(act, g_mm, A_G * b + t + 1)
                a.activation(g_h[:, 2 * t:2 * t + 2, :], key_bank[t][:, :].rearrange("p (h l) -> p h l", h=2),
                             ACT.Copy).then_inc(g_high, 1)

            def pT_copy(b, t):
                after(act, pT_mm, A_S * b + t + 1)
                if t == 0:
                    after(act, pv_mm, b)
                pT_places(a.copy, t).then_inc(pT_act, 1)

            def v_copy(b, q, t):
                after(act, v_mm, A_V * b + t + 1)
                a.activation(vals[q][:, t, :], key_bank[t][:, :], ACT.Copy).then_inc(v_copied, 1)

            def exp_sums(b, t):
                after(act, s_max, A_S * b + t + 1)
                if t == 0:
                    after(act, s_rec, 3 * b)
                after(act, pT_mm, A_S * (b - 1) + t + 1)
                jb, nk, nh, n = blocks_of(t)
                for i in range(nh):
                    a.activation(probs[:, t, nk * i:nk * i + nk], key_bank[(t + 2) % 4][:, nk * i:nk * i + nk],
                                 ACT.Exp, bias=negmax[:, jb, n + i:n + i + 1],
                                 accum_out=sums[:, jb, n + i:n + i + 1]).then_inc(s_sum, 1)

            def moe_copy(k):
                after(act, down_mm, k)
                after(act, moeT_mm, k - 1)
                a.activation(moe, moe_bank[:, :], ACT.Copy).then_inc(moe_copied, 1)

            def chunk(k):
                if isinstance(k, int) and k == NCH:
                    moe_copy(k)
                    return
                for p in range(4):
                    after(act, up_mm, 4 * k + p + 1)
                    after(act, weighted, 4 * (k - 1) + p + 1)
                    a.activation(hid[:, p, :], up_bank[p % 2][:, :], ACT.Gelu, bias=cw("b1")[:, p:p + 1]).then_inc(gelued, 1)
                    if p == 1 and not (isinstance(k, int) and k == 0):
                        moe_copy(k)

            def combT_copy(b):
                after(act, c_mm, b + 1)
                a.activation(combT[0:4 * E, bass.ds(L * b, L)], rout_bank[0:4 * E, 0:L], ACT.Copy).then_inc(c_copied, 1)

            def ys_copies(b):
                after(act, ys_mm, b + 1)
                a.activation(ys[:, :], rout_bank[:, 0:L], ACT.Copy).then_inc(ys_copied, 1)
                a.activation(ysall[:, bass.ds(L * b, L)], rout_bank[:, 0:L], ACT.Copy).then_inc(ys_copied, 1)

            def xs_copy(b, q):
                after(act, xs_mm, b + 1)
                a.activation(xs[q][:, :], norm_bank[:, 0:L], ACT.Copy).then_inc(xs_copied, 1)

            def proj_copy(b):
                after(act, pv_mm, b + 1)
                after(act, oT_mm, b)
                a.activation(proj[:, :], prob_bank[0][:, 0:L], ACT.Copy).then_inc(o_copied, 1)

            def step(s, q, on):
                def run(stage, piece, *args):
                    if on[stage]:
                        piece(s - stage, *args)
                r = 1 - q
                fill = isinstance(s, int) and s == 1
                if isinstance(s, int) and s == B + 1:
                    a.preload_act_table_set("gelu_and_others")
                for t in range(A_G):
                    run(1, g_high_part, t)
                run(2, pT_copy, 0)
                run(1, v_copy, r, 0)
                run(2, pT_copy, 1)
                run(1, v_copy, r, 1)
                if fill:
                    h1_part(5)
                    mixed_part(6)
                for t in range(2, 4):
                    run(2, pT_copy, t)
                if isinstance(s, int) and s == B + 1:
                    chunk(0)
                run(1, exp_sums, 0)
                if fill:
                    h1_part(6)
                    mixed_part(7)
                run(1, exp_sums, 1)
                run(2, pT_copy, 5)
                run(1, exp_sums, 2)
                if isinstance(s, int) and s == B + 2:
                    chunk(1)
                run(3, ys_copies)
                run(1, exp_sums, 3)
                if isinstance(s, int) and s == B + 3:
                    chunk(3)
                if isinstance(s, int) and s == B + 2:
                    chunk(2)
                run(4, combT_copy)
                run(0, xs_copy, q)
                if fill:
                    h1_part(7)
                for t in range(4, 6):
                    run(1, exp_sums, t)
                run(2, proj_copy)

            pipeline(act, step)

            chunks(act, chunk)

        @block.vector
        def _(dve):
            v = nc.vector
            for part in range(2):
                v.memset(xrows[P // 2:P, slice(*X_PARTS[part:part + 2])], 0.0).then_inc(zeroed, 1)
            v.memset(state[:, :, 0:1], 0.0).then_inc(edge_zero, 1)
            for c in range(NCH):
                dve.wait_ge(drive_mm, c + 1)
                v.tensor_copy(drive[:, CH * c:CH * c + CH], bank[c][:, :]).then_inc(drive_copied, 1)
            v.memset(combT[:, :].bitcast(F32), 0.0).then_inc(dve_consts, 1)
            dve.wait_ge(const_in, 16)
            v.tensor_copy(ident_bf[:, :], cw("ident")).then_inc(dve_consts, 1)

            def step_presum(t, c):
                dve.wait_ge(step_mm, NCH * t + c + 1)
                dve.wait_ge(state_ready, NCH * t + c + 5)
                v.tensor_tensor(presum[:, c % 4, :], bank[c][:, :], drive[:, CH * c:CH * c + CH], ALU.add).then_inc(step_sum, 1)

            with dve.Fori(0, STEPS - 2) as t:
                for c in range(NCH):
                    step_presum(t, c)
            t = STEPS - 2
            for c in range(NCH):
                if c >= 4 and c % 2 == 0:
                    dve.wait_ge(down_even, c // 2 - 1)
                elif c >= 4:
                    dve.wait_ge(down_odd, c // 2 - 1)
                step_presum(t, c)
                if c % 2 == 0:
                    dve.wait_ge(step_sum, NCH * t + c + 1)
                    v.tensor_scalar(state[D:P, seq2(c), L - 2::-1], two(presum[D:P, c % 4, :])[:, :, 0:L - 1], 0.0, None,
                                    ALU.max).then_inc(down_even, 1)

            def g_low_part(b, t):
                after(dve, g_high, A_G * b + t + 1)
                v.tensor_tensor(g_l[:, 2 * t:2 * t + 2, :], key_bank[t][:, :].rearrange("p (h l) -> p h l", h=2),
                                g_h[:, 2 * t:2 * t + 2, :].bitcast(F32), ALU.subtract).then_inc(g_low, 1)

            def pT_copy(b, t):
                after(dve, pT_mm, A_S * b + t + 1)
                if t == 4:
                    after(dve, pv_mm, b)
                pT_places(v.tensor_copy, t).then_inc(pT_dve, 1)

            def one_over_sums(b, t):
                jb, nk, nh, n = blocks_of(t)
                after(dve, s_sum, exps_done(b, t + 1))
                after(dve, s_scaled, A_S * (b - 1) + t + 2)
                v.reciprocal(rec[:, jb, n:n + 2 * nh], sums[:, jb, n:n + 2 * nh]).then_inc(s_rec, 1)

            def score_max(b, t):
                after(dve, s_mm, A_S * b + t + 1)
                jb, nk, nh, n = blocks_of(t)
                after(dve, s_sum, exps_done(b - 1, t))
                o, src = negmax[:, jb, n:n + nh], key_bank[(t + 2) % 4][:, :].rearrange("p (h l) -> p h l", h=nh)
                v.tensor_reduce(o, src, AX.X, ALU.max, negate=True).then_inc(s_max, 1)

            def moments(b, src, stat, s_stats):
                for t in range(2):
                    v.bn_stats(stat[:, t, :], src(t)).then_inc(s_stats, 1)

            def gathered(b, stat, s_stats, mom, s_moms):
                for t in range(2):
                    after(dve, s_stats, 2 * b + t + 1, apart=True)
                    v.bn_aggr(mom[:, t, :], stat[:, t, :]).then_inc(s_moms, 1)

            def normed(b, src, mom, s_rstd, rs, o, s_o):
                after(dve, s_rstd, b + 1)
                for t in range(2):
                    v.tensor_scalar(o[:, t, :], src(t), mom[:, t, 0:1], rs[:, t:t + 1], ALU.subtract,
                                    ALU.mult).then_inc(s_o, 1)

            def weights_low():
                dve.wait_ge(wg_h, 2)
                for i in range(2):
                    v.tensor_tensor(wg_low[:, :, i, :], prob_bank[0][:, :].rearrange("p (h d) -> p h d", h=H),
                                    wg_high[:, :, i, :].bitcast(F32), ALU.subtract).then_inc(wg_l, 1)
                dve.wait_ge(wv_h, 1)
                v.tensor_tensor(wv_low[:, :], prob_bank[1][:, :], wv_high[:, :].bitcast(F32),
                                ALU.subtract).then_inc(wv_l, 1)

            def leave(k):
                src = turn_bank[:, :].rearrange("p (t e) -> p t e", t=CH // P)
                after(dve, moeT_mm, k)
                v.tensor_tensor(outa, src[:, :, 0:D], base[:, bass.ds((k - 1) * (CH // P), CH // P), :],
                                ALU.add).then_inc(out_a, 1)
                after(dve, out_a, k)
                after(dve, out_dma, 16 * (k - 1))
                v.tensor_tensor(outb, src[:, :, D:P], outa, ALU.add).then_inc(out_b, 1)

            def weigh(k, pairs):
                for p in pairs:
                    after(dve, gelued, 4 * k + p + 1)
                    after(dve, wt_mm, 4 * k + p + 1)
                    after(dve, down_a if p < 2 else down_mm, k)
                    v.tensor_tensor(hidw[:, p, :], wt_bank[p % 2][:, :], hid[:, p, :], ALU.mult).then_inc(weighted, 1)

            def chunk(k):
                if not (isinstance(k, int) and k == NCH):
                    weigh(k, range(4))
                if not (isinstance(k, int) and k == 0):
                    leave(k)

            def residual(b):
                src = rout_bank[:, 0:2 * P].rearrange("p (t e) -> p t e", t=2)
                after(dve, oT_mm, b + 1)
                v.tensor_tensor(h2a[:, :, :], src[:, :, 0:D], h1[:, bass.ds(2 * b, 2), :], ALU.add).then_inc(r_h2a, 1)

            def residual_sum(b):
                src = rout_bank[:, 0:2 * P].rearrange("p (t e) -> p t e", t=2)
                after(dve, r_h2a, b + 1)
                after(dve, r_base, b)
                v.tensor_tensor(h2[:, :, :], src[:, :, D:P], h2a[:, :, :], ALU.add).then_inc(r_h2, 1)

            def second_stats(b):
                after(dve, r_h2, b + 1)
                moments(b, lambda t: h2[:, t, :], stat_r, r_stats)

            def second_moments(b):
                gathered(b, stat_r, r_stats, mom_r, r_moms)

            def second_norm(b):
                normed(b, lambda t: h2[:, t, :], mom_r, r_rstd, rstd_r, yn, r_yn)

            def second_high(b):
                after(dve, r_yn, 2 * b + 2)
                v.tensor_copy(rowy[:, :, D:2 * D], yn[:, :, :]).then_inc(r_high, 1)

            def second_low(b):
                after(dve, r_high, b + 1)
                v.tensor_tensor(rowy[:, :, 0:D], yn[:, :, :], rowy[:, :, D:2 * D].bitcast(F32),
                                ALU.subtract).then_inc(r_low, 1)

            def h1_rows(b):
                return lambda t: h1[:, bass.ds(2 * b + t, 1), :].rearrange("p o d -> p (o d)")

            def first_stats(b):
                if isinstance(b, int):
                    dve.wait_ge(h1_copied, b // 2 + 1 if b < 3 else NCH)
                moments(b, h1_rows(b), stat_n, n_stats)

            def first_moments(b):
                gathered(b, stat_n, n_stats, mom_n, n_moms)

            def first_norm(b):
                after(dve, n_low, b)
                normed(b, h1_rows(b), mom_n, n_rstd, rstd_n, xn, n_xn)

            def weights_sum(b):
                after(dve, lg_exp, b + 1)
                v.tensor_scalar(den[:, :], egap[:, :], 1.0, None, ALU.add).then_inc(lg_den, 1)

            def first_weight(b):
                after(dve, lg_den, b + 1)
                v.reciprocal(wts[:, :, 0], den[:, :]).then_inc(lg_w0, 1)

            def second_weight(b):
                after(dve, lg_w0, b + 1)
                v.tensor_tensor(wts[:, :, 1], egap[:, :], wts[:, :, 0], ALU.mult).then_inc(lg_w1, 1)

            def two_experts(b):
                after(dve, lg_mm, b + 1, apart=True)
                for t in range(2):
                    v.max(srt[:, t, :], rout_bank[:, E * t:E * t + E]).then_inc(lg_sorted, 1)

            def expert_index(b):
                for t in range(2):
                    after(dve, lg_sorted, 2 * b + t + 1, apart=True)
                    v.max_index(idx[:, t, :], srt[:, t, :], rout_bank[:, E * t:E * t + E]).then_inc(lg_index, 1)
                after(dve, lg_exp, b)
                v.tensor_tensor(gap[:, :], srt[:, :, 1], srt[:, :, 0], ALU.subtract).then_inc(lg_gap, 1)

            def one_hots(b):
                after(dve, lg_index, 2 * b + 2)
                after(dve, c_hotw, b)
                v.tensor_tensor(hot[:, :, :, :], cw("iota").unsqueeze(1).unsqueeze(1).broadcast_to([P, 2, 2, E]),
                                idx[:, :, 0:2].unsqueeze(3).broadcast_to([P, 2, 2, E]),
                                ALU.is_equal).then_inc(c_hot, 1)

            def step(s, q, on):
                def run(stage, piece, *args):
                    if on[stage]:
                        piece(s - stage, *args)
                if isinstance(s, int) and s == 0:
                    weights_low()
                run(0, first_stats)
                run(1, g_low_part, 0)
                run(0, first_moments)
                for t in range(1, 3):
                    run(1, g_low_part, t)
                run(3, residual)
                run(1, g_low_part, 3)
                run(3, residual_sum)
                run(3, second_stats)
                run(3, second_moments)
                run(1, score_max, 0)
                run(3, second_norm)
                run(1, score_max, 1)
                if isinstance(s, int) and s == B + 2:
                    weigh(1, (0, 1))
                if isinstance(s, int) and s == B + 1:
                    chunk(0)
                run(0, first_norm)
                run(3, second_high)
                run(4, weights_sum)
                run(3, second_low)
                run(4, first_weight)
                run(1, score_max, 2)
                run(2, pT_copy, 4)
                run(4, second_weight)
                if isinstance(s, int) and s == B + 2:
                    weigh(1, (2, 3))
                    leave(1)
                run(1, one_over_sums, 0)
                for t in range(3, 5):
                    run(1, score_max, t)
                run(1, one_over_sums, 2)
                run(1, score_max, 5)
                if isinstance(s, int) and s == B + 2:
                    chunk(2)
                run(3, two_experts)
                run(3, expert_index)
                run(1, one_over_sums, 4)
                run(3, one_hots)
                if isinstance(s, int) and s == B + 3:
                    chunk(3)

            pipeline(dve, step)

            chunks(dve, chunk)

        @block.tensor
        def _(pe):
            mm = nc.tensor.matmul
            ident = cw("ident")

            def tr(o, src):
                return nc.tensor.transpose(o, src.bitcast(F32), ident[0:src.shape[0], 0:src.shape[0]])

            pe.wait_ge(tok_in, 16)
            for c in range(NCH):
                if CH * c in X_PARTS:
                    part = X_PARTS.index(CH * c)
                    pe.wait_ge(x_in[part], 16)
                    pe.wait_ge(zeroed, part + 1)
                    pe.wait_ge(zeroed_low, part + 1)
                mm(bank[c][:, :], tw("wa"), xrows[:, CH * c:CH * c + CH], start=True, stop=True).then_inc(drive_mm, 1)
            pe.wait_ge(edge_zero, 1)
            with pe.Fori(0, STEPS - 1) as t:
                for c in range(NCH):
                    pe.wait_ge(state_ready, NCH * t + c + 1)
                    mm(bank[c][:, :], tw("w2"), state[:, seq2(c), 0:L], start=True, stop=True).then_inc(step_mm, 1)
            def heads_product(i):
                left, right = (("q", "k"), ("v", "o"))[i]
                lw = heads_w[:, slice(*M_AT[left])].rearrange("p (h e) -> p h e", h=H)
                rw = heads_w[:, slice(*M_AT[right])].rearrange("p (h e) -> p h e", h=H)
                pe.wait_ge(step_sum, NCH * (STEPS - 2) + 5 + i)
                for n in range(H):
                    last = mm(prob_bank[i][:, n * D:n * D + D], lw[:, n, :], rw[:, n, :], start=True, stop=True)
                last.then_inc(wg_mm, 1)

            def g_product(b, q, t):
                after(pe, s_sum, exps_done(b - 1, t + 2))
                for n in (2 * t, 2 * t + 1):
                    o = key_bank[t][:, L * (n % 2):L * (n % 2) + L]
                    mm(o, wg_high[:, n, :, :], xs[q][:, :], start=True, stop=False)
                    last = mm(o, wg_low[:, n, :, :], xs[q][:, :], start=False, stop=True)
                last.then_inc(g_mm, 1)

            def v_product(b, q, t):
                after(pe, g_low, A_G * b + t + 1)
                mm(key_bank[t][:, :], xs[q][:, P * t:P * t + P], wv_high[:, :], start=True, stop=False)
                mm(key_bank[t][:, :], xs[q][:, P * t:P * t + P], wv_low[:, :], start=False,
                   stop=True).then_inc(v_mm, 1)

            def score_product(b, q, t):
                if t < 2:
                    after(pe, g_low, A_G * b + 4)
                elif t < 4:
                    after(pe, v_copied, A_V * b + t - 1)
                else:
                    after(pe, s_sum, exps_done(b, t - 4))
                jb, nk, nh, n = blocks_of(t)
                o = key_bank[(t + 2) % 4][:, :].rearrange("p (h l) -> p h l", h=nh)
                mm(o, xs[q][:, P * jb:P * jb + P], g_h[:, n:n + nh, 0:nk], start=True, stop=False)
                mm(o, xs[q][:, P * jb:P * jb + P], g_l[:, n:n + nh, 0:nk], start=False, stop=False)
                mm(o[:, :, nk - P:nk], ident_bf[:, :], causal_bf[:, 0:nh, :], start=False, stop=True).then_inc(s_mm, 1)

            def prob_turn(b, t):
                if t == 0:
                    after(pe, o_copied, b)
                after(pe, s_scaled, A_S * b + t + 1)
                if t == 0:
                    after(pe, pT_dve, b)
                else:
                    after(pe, pT_act, 5 * b + t - 1)
                for i in range(CH // P):
                    last = tr(prob_bank[t % 2][:, P * i:P * i + P], probs[:, t, P * i:P * i + P])
                last.then_inc(pT_mm, 1)

            def value_product(b, q, grp):
                if grp == 0:
                    after(pe, pT_act, 5 * b + 5)
                    after(pe, pT_dve, b + 1)
                for n in range(HG * grp, HG * grp + HG, 2):
                    for kb in range(2):
                        for i in range(2):
                            last = mm(prob_bank[0][D * i:D * i + D, P * kb:L],
                                      vals[q][:, kb, D * (n + i):D * (n + i) + D],
                                      pt[:, n + i, L * kb:L * kb + L - P * kb], start=(n == 0 and kb == 0),
                                      stop=(n == H - 2 and kb == 1))
                if grp == 1:
                    last.then_inc(pv_mm, 1)

            def up(k, p):
                after(pe, gelued, 4 * k + p - 1)
                cols = bass.ds(CH * k, CH)
                mm(up_bank[p % 2][:, :], w1_high[:, P * p:P * p + P], ysall[:, cols], start=True, stop=False)
                mm(up_bank[p % 2][:, :], w1_low[:, P * p:P * p + P], ysall[:, cols], start=False,
                   stop=True).then_inc(up_mm, 1)
                after(pe, weighted, 4 * k + p - 1)
                mm(wt_bank[p % 2][:, :], sel[:, P * p:P * p + P], combT[:, cols], start=True, stop=True).then_inc(wt_mm, 1)

            def down(k, i):
                if i == 0:
                    after(pe, moe_copied, k)
                    mm(moe_bank[:, :], b2_parts[:, :], combT[:, bass.ds(CH * k, CH)], start=True, stop=False)
                after(pe, weighted, 4 * k + 2 * i + 2)
                for p in (2 * i, 2 * i + 1):
                    last = mm(moe_bank[D * (p % 2):D * (p % 2) + D, :], cw("w2e")[:, D * p:D * p + D], hidw[:, p, :],
                              start=False, stop=i == 1)
                last.then_inc(down_mm if i else down_a, 1)

            def turn(k):
                after(pe, moe_copied, k)
                after(pe, out_b, k - 1)
                for t in range(CH // P):
                    last = tr(turn_bank[:, P * t:P * t + P], moe[:, P * t:P * t + P])
                last.then_inc(moeT_mm, 1)

            def chunk(k):
                first = isinstance(k, int) and k == 0
                if isinstance(k, int) and k == NCH:
                    down(k - 1, 1)
                    turn(k)
                    return
                if first:
                    pe.wait_ge(s_sum, SUMS * B)
                    pe.wait_ge(xs_copied, B)
                if isinstance(k, int) and k == 1:
                    pe.wait_ge(pT_act, 5 * B)
                for p in range(4):
                    up(k, p)
                    if p == 1 and not first:
                        down(k - 1, 1)
                down(k, 0)
                if not first:
                    turn(k)

            def out_turn(b):
                after(pe, o_copied, b + 1)
                after(pe, lg_index, 2 * b)
                for t in range(2):
                    last = tr(rout_bank[:, P * t:P * t + P], proj[:, P * t:P * t + P])
                last.then_inc(oT_mm, 1)

            def ys_turn(b):
                after(pe, r_low, b + 1)
                after(pe, r_h2, b + 1)
                for t in range(2):
                    last = tr(rout_bank[:, P * t:P * t + P], rowy[:, t, :])
                last.then_inc(ys_mm, 1)

            def comb_turn(b, alone):
                after(pe, c_low, b + 1)
                after(pe, lg_index if alone else ys_copied, 2 * B if alone else 2 * (b + 2))
                for t in range(2):
                    last = tr(rout_bank[0:4 * E, P * t:P * t + P], rowc[:, t, :, :].rearrange("p r e -> p (r e)"))
                last.then_inc(c_mm, 1)

            def logits(b):
                after(pe, ys_copied, 2 * b + 2)
                after(pe, c_copied, b)
                for t in range(2):
                    o = rout_bank[:, E * t:E * t + E]
                    mm(o, ys[:, P * t:P * t + P], wr_high[:, :], start=True, stop=False)
                    last = mm(o, ys[:, P * t:P * t + P], wr_low[:, :], start=False, stop=True)
                last.then_inc(lg_mm, 1)

            def xs_turn(b):
                after(pe, n_low, b + 1)
                if isinstance(b, int) and b == 0:
                    pe.wait_ge(step_sum, NCH * (STEPS - 1) - 1)
                after(pe, xs_copied, b)
                for t in range(2):
                    last = tr(norm_bank[:, P * t:P * t + P], rowx[:, t, :])
                last.then_inc(xs_mm, 1)

            def step(s, q, on):
                def run(stage, piece, *args):
                    if on[stage]:
                        piece(s - stage, *args)
                r = 1 - q
                if isinstance(s, int) and s == 1:
                    pe.wait_ge(wg_l, 2)
                    pe.wait_ge(wv_l, 1)
                if on[1]:
                    after(pe, xs_copied, s)
                fill = isinstance(s, int) and s == 1
                for t in range(2):
                    run(1, g_product, r, t)
                run(3, out_turn)
                for t in range(2, 4):
                    run(1, g_product, r, t)
                if fill:
                    mixed_turn(5)
                run(2, prob_turn, 0)
                run(1, v_product, r, 0)
                run(2, prob_turn, 1)
                run(1, v_product, r, 1)
                if fill:
                    mixed(6)
                run(2, prob_turn, 2)
                run(1, score_product, r, 0)
                run(2, prob_turn, 3)
                run(1, score_product, r, 1)
                if fill:
                    mixed_turn(6)
                    mixed(7)
                for t in range(2, 4):
                    run(1, score_product, r, t)
                if isinstance(s, int) and s == B + 1:
                    chunk(0)
                run(2, prob_turn, 4)
                if isinstance(s, int) and s == B + 2:
                    chunk(1)
                run(2, prob_turn, 5)
                run(1, score_product, r, 4)
                run(3, ys_turn)
                if fill:
                    mixed_turn(7)
                run(1, score_product, r, 5)
                run(0, xs_turn)
                run(2, value_product, q, 0)
                if isinstance(s, int) and s == B + 3:
                    chunk(3)
                if isinstance(s, int) and s == B + 2:
                    chunk(2)
                run(4, comb_turn, not on[3])
                run(2, value_product, q, 1)
                run(3, logits)

            def mixed(c):
                if c == 0:
                    pe.wait_ge(down_edge, 1)
                pe.wait_ge(state_ready, NCH * (STEPS - 1) + c + 1)
                pe.wait_ge(down_odd if c % 2 else down_even, c // 2 + 1)
                if c < 4:
                    pe.wait_ge(step_sum, NCH * (STEPS - 2) + c + 1)
                elif c < M_FIRST:
                    pe.wait_ge(mixed_relu, c - 3)
                else:
                    pe.wait_ge(wg_l if c % 2 == 0 else wv_l, 2 if c % 2 == 0 else 1)
                for w, rows in ((tw("wc"), xrows), (tw("w4"), None)):
                    for i in range(2):
                        b = BPC * c + i
                        last = mm(mixed_bank(c)[D * i:D * i + D, 0:L], w,
                                  rows[:, L * b:L * b + L] if rows is not None else state[:, b, 0:L],
                                  start=rows is not None, stop=rows is None)
                last.then_inc(mixed_mm, 1)

            def mixed_turn(c):
                pe.wait_ge(mixed_relu, c + 1)
                if c == 0:
                    pe.wait_ge(step_sum, NCH * (STEPS - 1))
                else:
                    pe.wait_ge(h1_copied, c)
                for t in range(2):
                    last = tr(rout_bank[:, P * t:P * t + P], mixedT[:, c, P * t:P * t + P])
                last.then_inc(mixedT_mm, 1)

            pe.wait_ge(heads_in, 16)
            pe.wait_ge(const_in, 16)
            heads_product(0)
            mixed(0)
            mixed(1)
            mixed_turn(0)
            heads_product(1)
            for c in range(2, M_FIRST):
                mixed(c)
                mixed_turn(c - 1)
            pe.wait_ge(pool_consts, 3)
            pe.wait_ge(dve_consts, 2)
            pe.wait_ge(split_h, 5)
            pe.wait_ge(split_l, 4)
            pipeline(pe, step)

            chunks(pe, chunk)


def kernel(**inputs):
    import concourse.bacc as bacc
    from concourse.bass_utils import run_bass_kernel_spmd

    f = {k: np.asarray(v) for k, v in inputs.items()}
    z = lambda *shape: np.zeros(shape, np.float32)
    x = f["x"].transpose(1, 0, 2)
    xin = z(IN_ROWS, TOK)
    xin[0:2 * DIMS] = np.concatenate([x, x[:, :, ::-1]], 0).reshape(2 * DIMS, TOK)
    xin[ONE_ROW:ONE_ROW + 3] = 1.0

    wa = z(P, P)
    wa[0:DIMS, 0:D] = wa[DIMS:2 * DIMS, D:P] = f["L0_tok_W1"].T
    for i, name in enumerate(("L0_tok_b1", "L0_tok_b2")):
        wa[ONE_ROW + i] = np.concatenate([f[name], f[name]])
    w2 = z(P, P)
    w2[0:D, 0:D] = w2[D:P, D:P] = f["L0_tok_W2"].T
    wc = z(P, D)
    wc[0:DIMS] = f["L0_tok_W3"].T
    for i, name in enumerate(("L0_tok_b3", "L0_tok_b4", "L0_tok_b4")):
        wc[ONE_ROW + i] = f[name]
    w4 = np.concatenate([f["L0_tok_W4"].T] * 2, 0)
    wtok = np.concatenate([wa, w2, wc, w4], 1)

    q, k, v = (f[f"L0_attn_{n}_matrices"].transpose(2, 0, 1) for n in ("query", "key", "value_in"))
    o = f["L0_attn_value_out_matrices"].transpose(1, 0, 2)
    twice = lambda a: np.concatenate([a, a], 2)
    wheads = np.concatenate([a.reshape(D, -1) for a in (twice(q), k, twice(v), o)], 1)

    double = lambda a: np.concatenate([a, a], 0)
    w1 = double(f["L0_ffn_w1"].transpose(1, 0, 2).reshape(D, E * D))
    wr = double(f["L0_ffn_router_w"].T)
    sel = z(P, E // 2, 2, D)
    for e in range(E):
        sel[e, e // 2, e % 2] = sel[E + e, e // 2, e % 2] = 1.0
    b2 = z(P, P)
    b2[0:E, 0:D] = b2[E:2 * E, 0:D] = f["L0_ffn_b2"]
    b2l = z(P, P)
    b2l[2 * E:4 * E] = b2[0:2 * E]
    w2e = f["L0_ffn_w2"].reshape(E // 2, P, D).transpose(1, 0, 2).reshape(P, 4 * D)
    b1 = f["L0_ffn_b1"].reshape(E // 2, P).T
    iota = np.tile(np.arange(E, dtype=np.float32), (P, 1))
    parts = {"ident": np.eye(P, dtype=np.float32), "w1": w1, "sel": sel.reshape(P, -1), "b2": b2, "b2l": b2l, "w2e": w2e,
             "wr": wr, "b1": b1, "iota": iota}
    wconst = np.concatenate([parts[n] for n in C_COLS], 1)

    arrays = {n: np.ascontiguousarray(a) for n, a in
              {"xin": xin, "wtok": wtok, "wheads": wheads, "wconst": wconst}.items()}
    nc = bacc.Bacc("TRN2", target_bir_lowering=False, num_devices=1)
    args = [nc.dram_tensor(n, a.shape, F32, kind="ExternalInput").ap() for n, a in arrays.items()]
    out = nc.dram_tensor("out", (TOK, D), F32, kind="ExternalOutput").ap()
    audio_tower(nc, *args, out)
    r = run_bass_kernel_spmd(nc, [arrays], core_ids=[0])
    return r.results[0]["out"].reshape(B, L, D)
```
